# Optimizing a Trainium2 kernel written in Bass

```python
import numpy as np
import jax
import jax.numpy as jnp

def _softmax(x, axis=-1):
    return jax.nn.softmax(x, axis=axis)

def _gelu(x):
    return jax.nn.gelu(x, approximate=True)

def _silu(x):
    return jax.nn.silu(x)

def _sigmoid(x):
    return jax.nn.sigmoid(x)

def _layernorm(x, axis=-1, eps=1e-05):
    m = jnp.mean(x, axis=axis, keepdims=True)
    v = jnp.var(x, axis=axis, keepdims=True)
    return (x - m) / jnp.sqrt(v + eps)

def _scatter_add(tgt, idx, src, axis=0):
    return tgt.at[idx].add(src)

def _segment_sum(src, seg, n):
    return jax.ops.segment_sum(src, seg, n)
kernel_name = 'mk_gnn_resnorm_d2_gnn_r8_2f79fb'

def setup_inputs(seed: int=0):
    np.random.seed(seed)
    _w = jnp.asarray

    def _rec_inputs():
        import jax
        import jax.numpy as jnp
        _gk = jax.random.key(seed)
        x = -0.0001006 + 1 * jax.random.normal(jax.random.fold_in(_gk, 1), (6250, 96), jnp.float32)
        _s = jax.random.randint(jax.random.fold_in(_gk, 2), (50000,), 0, 6250, jnp.int32)
        _d = jax.random.randint(jax.random.fold_in(_gk, 3), (50000,), 0, 6250, jnp.int32)
        _loop = jnp.arange(6250, dtype=jnp.int32)
        src = jnp.concatenate([_s, _d, _loop])
        dst = jnp.concatenate([_d, _s, _loop])
        _o = jnp.argsort(dst, stable=True)
        src = src[_o]
        dst = dst[_o]
        edge_attr_96 = -4.21973e-06 + 0.0999841 * jax.random.normal(jax.random.fold_in(_gk, 12), (106250, 96), jnp.float32)
        return (x, src, dst, edge_attr_96)
    x, src, dst, edge_attr_96 = _rec_inputs()

    def _L0_gnn_setup():
        import jax, jax.numpy as jnp
        import numpy as np
        N_NODES = 6250
        N_EDGES = 100000
        HID = 96

        def _gelu(x):
            return jax.nn.gelu(x, approximate=False)
        key = jax.random.key(seed)
        ks = jax.random.split(key, 12)
        s = 1.0 / np.sqrt(HID)
        return {'x_feat': jax.random.normal(ks[0], (N_NODES, HID), jnp.float32), 'bases': jax.random.normal(ks[1], (N_EDGES, HID), jnp.float32) * 0.1, 'W_pre': jax.random.normal(ks[2], (HID, HID), jnp.float32) * s, 'b_pre': jax.random.normal(ks[3], (HID,), jnp.float32) * s, 'W1': jax.random.normal(ks[4], (HID, HID), jnp.float32) * s, 'b1': jax.random.normal(ks[5], (HID,), jnp.float32) * s, 'W2': jax.random.normal(ks[6], (HID, HID), jnp.float32) * s, 'b2': jax.random.normal(ks[7], (HID,), jnp.float32) * s, 'src': jax.random.randint(ks[8], (N_EDGES,), 0, N_NODES, jnp.int32), 'dst': jax.random.randint(ks[9], (N_EDGES,), 0, N_NODES, jnp.int32)}
    _L0_gnn_all = _L0_gnn_setup()
    _L0_gnn_in = {k: v for k, v in _L0_gnn_all.items() if k in ('W_pre', 'b_pre', 'W1', 'b1', 'W2', 'b2')}
    del _L0_gnn_all

    def _L1_gnn_setup():
        import jax, jax.numpy as jnp
        import numpy as np
        N_NODES = 6250
        N_EDGES = 100000
        D_IN = 96
        D_OUT = 96
        key = jax.random.key(seed)
        k1, k2, k3, k4, k5, k6 = jax.random.split(key, 6)
        x = jax.random.normal(k1, (N_NODES, D_IN), dtype=jnp.float32)
        edge_index = jax.random.randint(k2, (2, N_EDGES), 0, N_NODES, dtype=jnp.int32)
        W_lin = jax.random.normal(k3, (D_OUT, D_IN), dtype=jnp.float32) * 0.1
        b_lin = jax.random.normal(k4, (D_OUT,), dtype=jnp.float32) * 0.1
        W_root = jax.random.normal(k5, (D_OUT, D_IN), dtype=jnp.float32) * 0.1
        b_root = jax.random.normal(k6, (D_OUT,), dtype=jnp.float32) * 0.1
        return {'x': x, 'edge_index': edge_index, 'W_lin': W_lin, 'b_lin': b_lin, 'W_root': W_root, 'b_root': b_root}
    _L1_gnn_all = _L1_gnn_setup()
    _L1_gnn_in = {k: v for k, v in _L1_gnn_all.items() if k in ('W_lin', 'b_lin', 'W_root', 'b_root')}
    del _L1_gnn_all
    return {'x': x, 'src': src, 'dst': dst, 'edge_attr_96': edge_attr_96, 'L0_gnn_W_pre': _L0_gnn_in['W_pre'], 'L0_gnn_b_pre': _L0_gnn_in['b_pre'], 'L0_gnn_W1': _L0_gnn_in['W1'], 'L0_gnn_b1': _L0_gnn_in['b1'], 'L0_gnn_W2': _L0_gnn_in['W2'], 'L0_gnn_b2': _L0_gnn_in['b2'], 'L1_gnn_W_lin': _L1_gnn_in['W_lin'], 'L1_gnn_b_lin': _L1_gnn_in['b_lin'], 'L1_gnn_W_root': _L1_gnn_in['W_root'], 'L1_gnn_b_root': _L1_gnn_in['b_root']}

def reference(x, src, dst, edge_attr_96, L0_gnn_W_pre, L0_gnn_b_pre, L0_gnn_W1, L0_gnn_b1, L0_gnn_W2, L0_gnn_b2, L1_gnn_W_lin, L1_gnn_b_lin, L1_gnn_W_root, L1_gnn_b_root):
    import jax
    import jax.numpy as jnp

    def _L0_gnn_ref(x_feat, bases, W_pre, b_pre, W1, b1, W2, b2, src, dst):
        import jax, jax.numpy as jnp
        import numpy as np
        N_NODES = 6250
        N_EDGES = 100000
        HID = 96

        def _gelu(x):
            return jax.nn.gelu(x, approximate=False)
        n = x_feat.shape[0]
        h = _gelu(x_feat @ W_pre + b_pre)
        msg = h[src] * bases
        aggr = jax.ops.segment_sum(msg, dst, num_segments=n)
        x = x_feat + aggr
        y = _gelu(_gelu(x @ W1 + b1) @ W2 + b2)
        return x + y

    def _L1_gnn_ref(x, edge_index, W_lin, b_lin, W_root, b_root):
        import jax, jax.numpy as jnp
        import numpy as np
        N_NODES = 6250
        N_EDGES = 100000
        D_IN = 96
        D_OUT = 96
        src, dst = (edge_index[0], edge_index[1])
        n = x.shape[0]
        deg = jax.ops.segment_sum(jnp.ones(src.shape[0], dtype=x.dtype), dst, num_segments=n)
        dinv = jax.lax.rsqrt(jnp.maximum(deg, 1.0))
        norm = dinv[src] * dinv[dst]
        h = x @ W_lin.T + b_lin
        msgs = h[src] * norm[:, None]
        agg = jax.ops.segment_sum(msgs, dst, num_segments=n)
        out = agg + x @ W_root.T + b_root
        return jax.nn.relu(out)
    edge_index = jnp.stack([src, dst])
    x = _layernorm(x + _L0_gnn_ref(x, edge_attr_96, L0_gnn_W_pre, L0_gnn_b_pre, L0_gnn_W1, L0_gnn_b1, L0_gnn_W2, L0_gnn_b2, src, dst), axis=-1)
    x = _layernorm(x + _L1_gnn_ref(x, edge_index, L1_gnn_W_lin, L1_gnn_b_lin, L1_gnn_W_root, L1_gnn_b_root), axis=-1)
    return x

_drawn_inputs = setup_inputs


def setup_inputs(seed=0):
    import zlib

    import numpy as np

    out = dict(_drawn_inputs(seed))
    spreads = {}
    factors = {'L0_gnn_b_pre': 3.805}
    for name, (base, spread) in spreads.items():
        noise = np.random.default_rng([zlib.crc32(name.encode()), seed]).standard_normal(out[name].shape)
        drawn = base * np.exp(spread * noise) if base else spread * noise
        out[name] = jnp.asarray(drawn.astype(out[name].dtype))
    for name, factor in factors.items():
        out[name] = (out[name] * factor).astype(out[name].dtype)
    return out
```

```python
from contextlib import ExitStack

import concourse.bass as bass
from concourse import mybir

F32 = mybir.dt.float32
I32 = mybir.dt.int32
ALU = mybir.AluOpType
ACT = mybir.ActivationFunctionType
AX = mybir.AxisListType

P = 128
N_NODES, D = 6250, 96
N_EDGES = 106250
WIN = 128

TILES = 10
GROUP = P * TILES
GROUPS = N_EDGES // GROUP
TAIL = N_EDGES - GROUPS * GROUP
COLS = GROUPS * TILES + 1
assert 0 < TAIL <= P and GROUPS % 2 == 1

SLOTS = 2
SLOTS = 2
CT = 4
CN = CT * P
CHUNKS = -(-N_NODES // CN)
NP = CHUNKS * CN
NT = NP // P
FULL = N_NODES // P
REST = N_NODES - FULL * P
WINDOWS = -(-N_NODES // WIN)
assert CHUNKS % 2 == 1 and (FULL // CT) == CHUNKS - 1 and FULL % CT == 0
EPS = 1e-5


def build(nc, x, xT_in, src, dst, first, edge, W_pre, b_pre, W1, b1, W2, b2,
          WlinT, b_lin, WrootT, b_root, out):
    with ExitStack() as ctx:
        def sb(name, shape, dt=F32):
            return ctx.enter_context(nc.sbuf_tensor(name, shape, dt))

        def ps(name, shape):
            return ctx.enter_context(nc.psum_tensor(name, shape, F32))

        def sem(name):
            return ctx.enter_context(nc.semaphore(name))

        table = [nc.dram_tensor("table_h", (NP, D), F32).ap(),
                 nc.dram_tensor("table_t", (NP, D), F32).ap()]

        featT = sb("featT", [D + 1, NP])
        sumT = [sb("sumT0", [D + 1, NP + WIN]),
                sb("sumT1", [D, NP + WIN])]
        nat = sb("nat", [P, NT, D])
        stage = sb("stage", [P, NT, D])
        root = sb("root", [P, NT, D])
        gath = sb("gath", [P, 2, TILES, D])
        edg = sb("edg", [P, 2, TILES, D])
        msg = sb("msg", [P, 2, TILES, D + 1])
        onehot = sb("onehot", [P, 2, TILES, WIN])
        srcs = sb("srcs", [P, COLS], I32)
        dsts = sb("dsts", [P, COLS], I32)
        slot_idx = sb("slot_idx", [P, 2, TILES], I32)
        base = sb("base", [P, GROUPS + 1], I32)
        rel = sb("rel", [P, COLS])
        iota = sb("iota", [P, WIN])
        ident = sb("ident", [P, P])
        y1 = sb("y1", [D + 1, 2, CN])
        w_pre = sb("w_pre", [D + 1, D])
        w1 = sb("w1", [D, D])
        w2 = sb("w2", [D + 1, D])
        w_lin = sb("w_lin", [D + 1, D])
        w_root = sb("w_root", [D + 1, D])
        b1c = sb("b1c", [D, 1])
        bns = sb("bns", [P, NT, 6])
        mean = sb("mean", [P, NT])
        gap = sb("gap", [P, NT])
        gap_sq = sb("gap_sq", [P, NT])
        rstd = sb("rstd", [P, NT])
        deg = sb("deg", [P, NT])
        dinv = sb("dinv", [P, NT])
        extent = sb("extent", [P, 4])
        worst = sb("worst", [1, 1])
        flag = sb("flag", [1, 1], I32)
        left = sb("left", [P, COLS])
        left_t = sb("left_t", [P, COLS])
        left_w = sb("left_w", [P, TILES])
        win_start = sb("win_start", [P, WINDOWS])

        seg = ps("seg", [P, 2, 512])
        bigA = ps("bigA", [P, 2, 512])
        bigB = ps("bigB", [P, 2, 512])
        bigC = ps("bigC", [P, 512])
        iota_ps = ps("iota_ps", [P, 512])

        s_pad = sem("s_pad")
        s_init = sem("s_init")
        s_const = sem("s_const")
        s_identz = sem("s_identz")
        s_x = sem("s_x")
        s_wpre = sem("s_wpre")
        s_idx_in = sem("s_idx_in")
        s_nat = sem("s_nat")
        s_w = sem("s_w")
        s_rel = sem("s_rel")
        s_ext = sem("s_ext")
        s_extT = sem("s_extT")
        s_flag = sem("s_flag")
        s_hmm = sem("s_hmm")
        s_h = sem("s_h")
        s_tab = [sem("s_tab0"), sem("s_tab1")]
        s_slot = [sem("s_slot0"), sem("s_slot1")]
        s_gath = [[sem(f"s_gath{r}_{s}") for s in range(SLOTS)] for r in range(2)]
        s_edge = [sem(f"s_edge{s}") for s in range(SLOTS)]
        s_go = sem("s_go")
        s_msg = sem("s_msg")
        s_oh = [sem("s_oh0"), sem("s_oh1")]
        s_seg = [sem("s_seg0"), sem("s_seg1")]
        s_add = [sem("s_add0"), sem("s_add1")]
        s_left = sem("s_left")
        s_lidx = [sem("s_lidx0"), sem("s_lidx1")]
        s_lgath = [sem("s_lgath0"), sem("s_lgath1")]
        s_ledge = sem("s_ledge")
        s_lmsg = sem("s_lmsg")
        s_lrel = [sem("s_lrel0"), sem("s_lrel1")]
        s_loh = [sem("s_loh0"), sem("s_loh1")]
        s_lseg = [sem("s_lseg0"), sem("s_lseg1")]
        s_ladd = [sem("s_ladd0"), sem("s_ladd1")]
        s_x1 = sem("s_x1")
        s_y1mm = sem("s_y1mm")
        s_y1 = sem("s_y1")
        s_y2mm = sem("s_y2mm")
        s_y2 = sem("s_y2")
        s_x1n = sem("s_x1n")
        s_zx = sem("s_zx")
        s_z = sem("s_z")
        s_stat = sem("s_stat")
        s_mv = sem("s_mv")
        s_clamp = sem("s_clamp")
        s_sqrt = sem("s_sqrt")
        s_rs = sem("s_rs")
        s_x2 = sem("s_x2")
        s_x2t = sem("s_x2t")
        s_x2T = sem("s_x2T")
        s_tmm = sem("s_tmm")
        s_t = sem("s_t")
        s_rmm = sem("s_rmm")
        s_root = sem("s_root")
        s_aggn = sem("s_aggn")
        s_f1 = sem("s_f1")
        s_f2 = sem("s_f2")
        s_f3 = sem("s_f3")
        s_fstat = sem("s_fstat")
        s_fmv = sem("s_fmv")
        s_fvar = sem("s_fvar")
        s_fsqrt = sem("s_fsqrt")
        s_frs = sem("s_frs")
        s_y = sem("s_y")
        s_out = sem("s_out")

        edge_g = edge[0:GROUPS * GROUP, :].rearrange("(g p j) d -> g p (j d)", p=P, j=TILES)
        edge_tail = edge[GROUPS * GROUP:N_EDGES, :]
        HALF = GROUPS // 2

        def pairs(eng, count, body):
            with eng.Fori(0, count // 2) as i:
                body(2 * i, 0)
                body(2 * i + 1, 1)
            body(count - 1, 0)

        def ahead(eng, early, late):
            early(0, 0)
            with eng.Fori(0, CHUNKS // 2) as i:
                early(2 * i + 1, 1)
                late(2 * i, 0)
                early(2 * i + 2, 0)
                late(2 * i + 1, 1)
            late(CHUNKS - 1, 0)

        def written_out(early, late):
            if early:
                early(0, 0)
            for c in range(CHUNKS):
                if early and c + 1 < CHUNKS:
                    early(c + 1, (c + 1) % SLOTS)
                late(c, c % SLOTS)

        def nodes_of(c):
            return bass.ds(c * CN, CN)

        def tile_nodes(c, t):
            return bass.ds(c * CN + t * P, P)

        def tiles_of(c):
            return bass.ds(c * CT, CT)

        def chunk_of(nat_like, c):
            return nat_like[:, tiles_of(c), :].rearrange("p t d -> p (t d)")

        def rows_of(tab, c):
            return tab[bass.ds(c * CN, CN), :].rearrange("(t p) d -> p t d", p=P)

        def bank3(bank, d=D):
            return bank[:, 0:CT * d].rearrange("p (t d) -> p t d", d=d)

        def left_flag(eng, at):
            eng.wait_ge(s_flag, 1)
            reg = eng.alloc_register(f"left_flag_{at}")
            eng.reg_load(reg, flag[0:1, 0:1])
            return reg

        block = ctx.enter_context(nc.Block())

        @block.sync
        def _(sp):
            sp.wait_ge(s_pad, 3)
            sp.dma_start(featT[0:D, 0:N_NODES], xT_in).then_inc(s_x, 16)
            sp.dma_start(nat[:, 0:FULL, :], x[0:FULL * P, :].rearrange("(t p) d -> p t d", p=P)
                         ).then_inc(s_nat, 16)
            sp.dma_start(nat[0:REST, FULL, :], x[FULL * P:N_NODES, :]).then_inc(s_nat, 16)
            for dst_tile, src_ap in ((w1[:], W1), (b1c[:], b1),
                                     (w2[0:D, :], W2), (w2[D:D + 1, :], b2),
                                     (w_lin[0:D, :], WlinT), (w_lin[D:D + 1, :], b_lin),
                                     (w_root[0:D, :], WrootT), (w_root[D:D + 1, :], b_root)):
                sp.dma_start(dst_tile, src_ap).then_inc(s_w, 16)

            def store_h(c, s):
                sp.wait_ge(s_h, c + 1 + SLOTS)
                sp.dma_start(rows_of(table[0], c), stage[:, tiles_of(c), :]).then_inc(s_tab[0], 16)

            pairs(sp, CHUNKS, store_h)

            def load_edges(g, s):
                sp.wait_ge(s_msg, g + 1)
                sp.dma_start(edg[:, s].rearrange("p j d -> p (j d)"),
                             edge_g[bass.ds(g, 1)].rearrange("g p f -> (g p) f")).then_inc(s_edge[s], 16)

            pairs(sp, GROUPS, load_edges)
            sp.wait_ge(s_msg, GROUPS + 1)
            sp.dma_start(edg[0:TAIL, 1, 0, :], edge_tail).then_inc(s_edge[1], 16)

            with sp.If_ne(left_flag(sp, 0), 0):
                with sp.Fori(0, GROUPS) as g:
                    sp.wait_ge(s_lmsg, g + 1)
                    sp.dma_start(edg[:, 0].rearrange("p j d -> p (j d)"),
                                 edge_g[bass.ds(g, 1)].rearrange("g p f -> (g p) f")
                                 ).then_inc(s_ledge, 16)
                sp.wait_ge(s_lmsg, GROUPS + 1)
                sp.dma_start(edg[0:TAIL, 0, 0, :], edge_tail).then_inc(s_ledge, 16)

            def store_t(c, s):
                sp.wait_ge(s_t, c + 1 + SLOTS)
                sp.dma_start(rows_of(table[1], c), stage[:, tiles_of(c), :]).then_inc(s_tab[1], 16)

            pairs(sp, CHUNKS, store_t)

            with sp.Fori(0, CHUNKS - 1) as c:
                sp.wait_ge(s_y, c + 1)
                sp.dma_start(rows_of(out, c), stage[:, tiles_of(c), :]).then_inc(s_out, 16)
            sp.wait_ge(s_y, CHUNKS)
            sp.dma_start(out[FULL * P:N_NODES, :], stage[0:REST, FULL, :]).then_inc(s_out, 16)
            sp.wait_ge(s_out, 16 * CHUNKS)

        @block.gpsimd
        def _(pool):
            pool.iota(iota[:], [[1, WIN]], base=0, channel_multiplier=0,
                      allow_small_or_imprecise_dtypes=True).then_inc(s_const, 1)
            pool.memset(ident[:], 0.0).then_inc(s_identz, 1)
            pool.wait_ge(s_identz, 1)
            pool.affine_select(out=ident[:], in_=ident[:], compare_op=ALU.not_equal, fill=1.0, base=0,
                               pattern=[[-1, P]], channel_multiplier=1).then_inc(s_const, 1)
            pool.iota(win_start[:], [[WIN, WINDOWS]], base=0, channel_multiplier=0,
                      allow_small_or_imprecise_dtypes=True).then_inc(s_const, 1)

            for r in range(2):
                rows_used = (s_msg, s_seg[1])[r]

                def gather(g, s, r=r, rows_used=rows_used):
                    pool.wait_ge(rows_used, g + 1)
                    pool.wait_ge(s_slot[r], g + 1)
                    pool.sem_inc(s_go, 1)
                    for j in range(TILES):
                        pool.indirect_dma_start(
                            gath[:, s, j, :], None, table[r],
                            bass.IndirectOffsetOnAxis(ap=slot_idx[:, s, j:j + 1], axis=0)
                        ).then_inc(s_gath[r][s], 16)

                pool.wait_ge(s_tab[r], 16 * CHUNKS)
                pairs(pool, GROUPS, gather)
                pool.wait_ge(rows_used, GROUPS + 1)
                pool.wait_ge(s_slot[r], GROUPS + 1)
                pool.indirect_dma_start(
                    gath[0:TAIL, 1, 0, :], None, table[r],
                    bass.IndirectOffsetOnAxis(ap=slot_idx[0:TAIL, 1, 0:1], axis=0)
                ).then_inc(s_gath[r][1], 16)

                with pool.If_ne(left_flag(pool, r), 0):
                    with pool.Fori(0, GROUPS) as g:
                        pool.wait_ge(s_lidx[r], g + 1)
                        pool.sem_inc(s_go, 1)
                        for j in range(TILES):
                            pool.indirect_dma_start(
                                gath[:, 0, j, :], None, table[r],
                                bass.IndirectOffsetOnAxis(ap=slot_idx[:, 0, j:j + 1], axis=0)
                            ).then_inc(s_lgath[r], 16)
                    pool.wait_ge(s_lidx[r], GROUPS + 1)
                    pool.indirect_dma_start(
                        gath[0:TAIL, 0, 0, :], None, table[r],
                        bass.IndirectOffsetOnAxis(ap=slot_idx[0:TAIL, 0, 0:1], axis=0)
                    ).then_inc(s_lgath[r], 16)

        def between_act(act):
            act.sem_inc(s_y1, SLOTS)
            act.sem_inc(s_y2, SLOTS)
            act.sem_inc(s_x2T, SLOTS)
            act.sem_inc(s_root, 1)
            act.wait_ge(s_w, 8 * 16)
            act.wait_ge(s_tab[0], 16 * CHUNKS)

            def hidden(c, s):
                act.wait_ge(s_y1mm, c + 1)
                act.wait_ge(s_y2mm, c + 1)
                act.activation(y1[0:D, s, :], bigA[0:D, s, :], ACT.Gelu, bias=b1c[:, 0:1]
                               ).then_inc(s_y1, 1)
                act.wait_ge(s_y2mm, c + 1 + SLOTS)
                act.activation(chunk_of(stage, c), bigB[:, s, 0:CT * D], ACT.Gelu).then_inc(s_y2, 1)

            pairs(act, CHUNKS, hidden)

            act.wait_ge(s_clamp, 2)
            act.activation(rstd[:], rstd[:], ACT.Sqrt).then_inc(s_sqrt, 1)
            act.activation(dinv[:], deg[:], ACT.Sqrt).then_inc(s_sqrt, 1)

            def turned(c, s):
                act.wait_ge(s_x2t, c + 1)
                act.copy(featT[0:D, nodes_of(c)], bigA[0:D, s, :]).then_inc(s_x2T, 1)
                act.wait_ge(s_rmm, c + 1)
                act.copy(chunk_of(root, c), bigC[:, 0:CT * D]).then_inc(s_root, 1)

            pairs(act, CHUNKS, turned)

        @block.scalar
        def _(act):
            act.dma_start(w_pre[0:D, :], W_pre).then_inc(s_wpre, 16)
            act.dma_start(w_pre[D:D + 1, :], b_pre).then_inc(s_wpre, 16)
            act.dma_start(srcs[:, 0:COLS - 1], src[0]).then_inc(s_idx_in, 16)
            act.dma_start(dsts[:, 0:COLS - 1], dst[0]).then_inc(s_idx_in, 16)
            act.dma_start(base[:], first.partition_broadcast(P)).then_inc(s_idx_in, 16)
            act.wait_ge(s_pad, 3)
            act.dma_start(srcs[0:TAIL, COLS - 1:COLS], src[1]).then_inc(s_idx_in, 16)
            act.dma_start(dsts[0:TAIL, COLS - 1:COLS], dst[1]).then_inc(s_idx_in, 16)
            act.sem_inc(s_h, SLOTS)

            def gelu_h(c, s):
                act.wait_ge(s_hmm, c + 1)
                act.activation(chunk_of(stage, c), bigB[:, s, 0:CT * D], ACT.Gelu).then_inc(s_h, 1)

            pairs(act, CHUNKS, gelu_h)

            act.wait_ge(s_idx_in, 5 * 16)
            for r in range(2):
                for s in range(SLOTS):
                    act.copy(slot_idx[:, s, :], srcs[:, s * TILES:(s + 1) * TILES]).then_inc(s_slot[r], 1)
                with act.Fori(1, HALF) as i:
                    for s in range(SLOTS):
                        act.wait_ge(s_gath[r][s], 16 * TILES * i)
                        act.copy(slot_idx[:, s, :], srcs[:, bass.ds((2 * i + s) * TILES, TILES)]
                                 ).then_inc(s_slot[r], 1)
                act.wait_ge(s_gath[r][0], 16 * TILES * HALF)
                act.copy(slot_idx[:, 0, :], srcs[:, (GROUPS - 1) * TILES:GROUPS * TILES]
                         ).then_inc(s_slot[r], 1)
                act.wait_ge(s_gath[r][1], 16 * TILES * HALF)
                act.copy(slot_idx[0:TAIL, 1, 0:1], srcs[0:TAIL, COLS - 1:COLS]).then_inc(s_slot[r], 1)

                with act.If_ne(left_flag(act, r), 0):
                    with act.Fori(0, GROUPS) as g:
                        act.wait_ge(s_ladd[r], g * WINDOWS + 1)
                        act.copy(slot_idx[:, 0, :], srcs[:, bass.ds(g * TILES, TILES)]
                                 ).then_inc(s_lidx[r], 1)
                    act.wait_ge(s_ladd[r], GROUPS * WINDOWS + 1)
                    act.copy(slot_idx[0:TAIL, 0, 0:1], srcs[0:TAIL, COLS - 1:COLS]
                             ).then_inc(s_lidx[r], 1)

                if r == 0:
                    between_act(act)

            act.wait_ge(s_fvar, 1)
            act.activation(rstd[:], rstd[:], ACT.Sqrt).then_inc(s_fsqrt, 1)

        def leftover_dve(dve, r, rows):
            with dve.If_ne(left_flag(dve, r), 0):
                if r == 0:
                    dve.tensor_scalar(left[:], rel[:], float(WIN), None, ALU.is_ge)
                    dve.tensor_scalar(left_t[:], rel[:], 0.0, None, ALU.is_lt).then_inc(s_left, 1)
                    dve.wait_ge(s_left, 1)
                    dve.tensor_tensor(left[:], left[:], left_t[:], ALU.add).then_inc(s_left, 1)
                    dve.wait_ge(s_left, 2)
                    dve.tensor_scalar(left_t[:], dsts[:], 1.0, None, ALU.add).then_inc(s_left, 1)
                    dve.wait_ge(s_left, 3)
                    dve.tensor_tensor(left[:], left[:], left_t[:], ALU.mult).then_inc(s_left, 1)
                    dve.wait_ge(s_left, 4)
                    dve.tensor_scalar(left[:], left[:], -1.0, None, ALU.add).then_inc(s_left, 1)
                    dve.wait_ge(s_left, 5)
                    dve.sem_inc(s_lmsg, 1)
                dve.sem_inc(s_ladd[r], 1)

                def left_group(g, k, tiles):
                    if r == 0:
                        dve.wait_ge(s_lgath[0], g * (16 * TILES) + 16 * tiles)
                        dve.wait_ge(s_ledge, g * 16 + 16)
                        dve.wait_ge(s_ladd[0], g * WINDOWS + 1)
                        dve.tensor_tensor(msg[0:k, 0, 0:tiles, 0:D], gath[0:k, 0, 0:tiles],
                                          edg[0:k, 0, 0:tiles], ALU.mult).then_inc(s_lmsg, 1)
                    with dve.Fori(0, WINDOWS) as w:
                        dve.wait_ge(s_ladd[r], g * WINDOWS + w + 1)
                        dve.tensor_scalar(left_w[0:k, 0:tiles], left[0:k, bass.ds(g * TILES, tiles)],
                                          win_start[0:k, bass.ds(w, 1)], None, ALU.subtract
                                          ).then_inc(s_lrel[r], 1)
                        dve.wait_ge(s_lrel[r], g * WINDOWS + w + 1)
                        dve.tensor_tensor(
                            onehot[0:k, 0, 0:tiles],
                            iota_ps[0:k, 0:WIN].unsqueeze(1).to_broadcast([k, tiles, WIN]),
                            left_w[0:k, 0:tiles].unsqueeze(2).to_broadcast([k, tiles, WIN]),
                            ALU.is_equal).then_inc(s_loh[r], 1)
                        dve.wait_ge(s_lseg[r], g * WINDOWS + w + 1)
                        dve.tensor_tensor(sumT[r][0:rows, bass.ds(w * WIN, WIN)],
                                          sumT[r][0:rows, bass.ds(w * WIN, WIN)],
                                          seg[0:rows, 0, 0:WIN], ALU.add).then_inc(s_ladd[r], 1)

                with dve.Fori(0, GROUPS) as g:
                    left_group(g, P, TILES)
                left_group(GROUPS, TAIL, 1)
                dve.wait_ge(s_ladd[r], (GROUPS + 1) * WINDOWS + 1)

        def tile_stats(dve, c, ready, done):
            dve.wait_ge(ready, c + 1)
            for t in range(CT):
                ins = dve.bn_stats(bns[:, bass.ds(c * CT + t, 1), :].rearrange("p a b -> p (a b)"),
                                   nat[:, bass.ds(c * CT + t, 1), :].rearrange("p a b -> p (a b)"))
            ins.then_inc(done, 1)

        def mean_and_var(dve, stats_done, step, done):
            dve.wait_ge(stats_done, CHUNKS)
            even, odd, dev_even, dev_odd = bns[:, :, 1], bns[:, :, 4], bns[:, :, 2], bns[:, :, 5]
            dve.tensor_tensor(mean[:], even, odd, ALU.add)
            dve.tensor_tensor(gap[:], even, odd, ALU.subtract)
            dve.tensor_tensor(rstd[:], dev_even, dev_odd, ALU.add).then_inc(step, 1)
            dve.wait_ge(step, 1)
            dve.tensor_scalar(mean[:], mean[:], 0.5, None, ALU.mult)
            dve.scalar_tensor_tensor(out=gap_sq[:], in0=gap[:], scalar=0.25, in1=gap[:],
                                     op0=ALU.mult, op1=ALU.mult)
            dve.tensor_scalar(rstd[:], rstd[:], 1.0 / D, EPS, ALU.mult, ALU.add).then_inc(step, 1)
            dve.wait_ge(step, 2)
            dve.tensor_tensor(rstd[:], rstd[:], gap_sq[:], ALU.add).then_inc(done, 1)

        def normalise(dve, c, to, done):
            for t in range(CT):
                k = bass.ds(c * CT + t, 1)
                ins = dve.tensor_scalar(to[:, k, :].rearrange("p a b -> p (a b)"),
                                        nat[:, k, :].rearrange("p a b -> p (a b)"),
                                        mean[:, k], rstd[:, k], ALU.subtract, ALU.mult)
            ins.then_inc(done, 1)

        def between_dve(dve):
            with dve.Fori(0, CHUNKS) as c:
                dve.tensor_tensor(sumT[0][0:D, nodes_of(c)], sumT[0][0:D, nodes_of(c)],
                                  featT[0:D, nodes_of(c)], ALU.add).then_inc(s_x1, 1)

            dve.wait_ge(s_nat, 32)

            def residual(c, s):
                dve.wait_ge(s_x1n, c + 1)
                dve.tensor_tensor(nat[:, tiles_of(c), :], nat[:, tiles_of(c), :],
                                  bank3(bigC, D + 1)[:, :, 0:D], ALU.add)
                dve.tensor_copy(deg[:, tiles_of(c)], bank3(bigC, D + 1)[:, :, D]).then_inc(s_zx, 1)
                dve.wait_ge(s_zx, c + 1 + 1)
                dve.wait_ge(s_y2, c + 1 + SLOTS)
                dve.tensor_tensor(chunk_of(nat, c), chunk_of(nat, c), chunk_of(stage, c), ALU.add
                                  ).then_inc(s_z, 1)
                tile_stats(dve, c, s_z, s_stat)

            pairs(dve, CHUNKS, residual)
            mean_and_var(dve, s_stat, s_mv, s_clamp)
            dve.tensor_scalar(deg[:], deg[:], 1.0, None, ALU.max).then_inc(s_clamp, 1)
            dve.wait_ge(s_sqrt, 2)
            dve.reciprocal(rstd[:], rstd[:]).then_inc(s_rs, 1)
            dve.reciprocal(dinv[:], dinv[:]).then_inc(s_rs, 1)
            dve.wait_ge(s_rs, 2)

            def layer_out(c, s):
                normalise(dve, c, nat, s_x2)

            def scale_t(c, s):
                dve.wait_ge(s_tmm, c + 1)
                dve.tensor_tensor(stage[:, tiles_of(c), :], bank3(bigB[:, s]),
                                  dinv[:, tiles_of(c)].unsqueeze(2).to_broadcast([P, CT, D]),
                                  ALU.mult).then_inc(s_t, 1)

            ahead(dve, layer_out, scale_t)

        def final_dve(dve):
            dve.wait_ge(s_tab[1], 16 * CHUNKS)
            dve.wait_ge(s_root, CHUNKS + 1)

            def combine(c, s):
                dve.wait_ge(s_aggn, c + 1)
                dve.tensor_tensor(stage[:, tiles_of(c), :], bank3(bigB[:, s]),
                                  dinv[:, tiles_of(c)].unsqueeze(2).to_broadcast([P, CT, D]),
                                  ALU.mult).then_inc(s_f1, 1)
                dve.wait_ge(s_f1, c + 1 + SLOTS)
                dve.tensor_tensor(chunk_of(stage, c), chunk_of(stage, c), chunk_of(root, c), ALU.add
                                  ).then_inc(s_f2, 1)
                dve.wait_ge(s_f2, c + 1)
                dve.scalar_tensor_tensor(out=chunk_of(nat, c), in0=chunk_of(stage, c), scalar=0.0,
                                         in1=chunk_of(nat, c), op0=ALU.max, op1=ALU.add
                                         ).then_inc(s_f3, 1)
                tile_stats(dve, c, s_f3, s_fstat)

            pairs(dve, CHUNKS, combine)
            mean_and_var(dve, s_fstat, s_fmv, s_fvar)
            dve.wait_ge(s_fsqrt, 1)
            dve.reciprocal(rstd[:], rstd[:]).then_inc(s_frs, 1)
            dve.wait_ge(s_frs, 1)
            with dve.Fori(0, CHUNKS) as c:
                normalise(dve, c, stage, s_y)

        @block.vector
        def _(dve):
            dve.memset(featT[:, N_NODES:NP], 0.0).then_inc(s_pad, 1)
            dve.memset(srcs[:, COLS - 1:COLS], 0)
            dve.memset(dsts[:, COLS - 1:COLS], 0).then_inc(s_pad, 1)
            dve.memset(nat[:, FULL:NT, :], 0.0).then_inc(s_pad, 1)
            dve.wait_ge(s_pad, 1)
            dve.memset(featT[D:D + 1, :], 1.0).then_inc(s_init, 1)
            dve.memset(msg[:, :, :, D:D + 1], 1.0)
            dve.memset(y1[D:D + 1, :, :], 1.0)
            dve.memset(sumT[0][:], 0.0)
            dve.memset(sumT[1][:], 0.0).then_inc(s_init, 1)
            dve.wait_ge(s_const, 3)
            dve.tensor_copy(iota_ps[:, 0:WIN], iota[:]).then_inc(s_init, 1)

            dve.wait_ge(s_idx_in, 5 * 16)
            dve.tensor_tensor(
                rel[:, 0:COLS - 1].rearrange("p (g j) -> p g j", j=TILES),
                dsts[:, 0:COLS - 1].rearrange("p (g j) -> p g j", j=TILES),
                base[:, 0:GROUPS].unsqueeze(2).to_broadcast([P, GROUPS, TILES]),
                ALU.subtract)
            dve.memset(rel[:, COLS - 1:COLS], 0.0).then_inc(s_rel, 1)
            dve.wait_ge(s_rel, 1)
            dve.tensor_tensor(rel[0:TAIL, COLS - 1:COLS], dsts[0:TAIL, COLS - 1:COLS],
                              base[0:TAIL, GROUPS:GROUPS + 1], ALU.subtract).then_inc(s_rel, 1)
            dve.wait_ge(s_rel, 2)
            dve.tensor_reduce(extent[:, 0:1], rel[:], AX.X, ALU.max)
            dve.tensor_reduce(extent[:, 1:2], rel[:], AX.X, ALU.min).then_inc(s_ext, 1)
            dve.wait_ge(s_ext, 1)
            dve.tensor_scalar(extent[:, 2:3], extent[:, 0:1], -float(WIN - 1), None, ALU.add)
            dve.tensor_scalar(extent[:, 3:4], extent[:, 1:2], -1.0, None, ALU.mult).then_inc(s_ext, 1)
            dve.wait_ge(s_extT, 1)
            dve.tensor_reduce(worst[:], bigC[0:1, 0:2 * P], AX.X, ALU.max).then_inc(s_ext, 1)
            dve.wait_ge(s_ext, 3)
            dve.tensor_scalar(flag[:], worst[:], 0.0, None, ALU.is_gt).then_inc(s_flag, 1)

            dve.sem_inc(s_msg, SLOTS)
            dve.sem_inc(s_add[0], SLOTS)
            dve.sem_inc(s_add[1], SLOTS)
            dve.sem_inc(s_zx, 1)
            dve.sem_inc(s_t, SLOTS)
            dve.sem_inc(s_f1, SLOTS)
            dve.wait_ge(s_init, 3)

            def add_window(g, s, r, rows):
                b = dve.value_load(base[0:1, bass.ds(g, 1)], min_val=0, max_val=N_NODES - 1)
                dve.wait_ge(s_seg[r], g + 1 + SLOTS)
                dve.wait_ge(s_add[r], g + SLOTS)
                dve.tensor_tensor(sumT[r][0:rows, bass.ds(b, WIN)], sumT[r][0:rows, bass.ds(b, WIN)],
                                  seg[0:rows, s, 0:WIN], ALU.add).then_inc(s_add[r], 1)

            for r in range(2):
                rows = (D + 1, D)[r]

                def group(g, s, r=r, rows=rows):
                    dve.wait_ge(s_seg[r], g + 1)
                    dve.tensor_tensor(
                        onehot[:, s], iota_ps[:, 0:WIN].unsqueeze(1).to_broadcast([P, TILES, WIN]),
                        rel[:, bass.ds(g * TILES, TILES)].unsqueeze(2).to_broadcast([P, TILES, WIN]),
                        ALU.is_equal).then_inc(s_oh[r], 1)
                    if r == 0:
                        dve.wait_ge(s_gath[0][s], (g - s) * (8 * TILES) + 16 * TILES)
                        dve.wait_ge(s_edge[s], (g - s) * 8 + 16)
                        dve.tensor_tensor(msg[:, s, :, 0:D], gath[:, s], edg[:, s], ALU.mult
                                          ).then_inc(s_msg, 1)
                    add_window(g, s, r, rows)

                pairs(dve, GROUPS, group)

                dve.wait_ge(s_seg[r], GROUPS + 1)
                dve.tensor_tensor(onehot[0:TAIL, 1, 0, :], iota_ps[0:TAIL, 0:WIN],
                                  rel[0:TAIL, COLS - 1:COLS].to_broadcast([TAIL, WIN]),
                                  ALU.is_equal).then_inc(s_oh[r], 1)
                if r == 0:
                    dve.wait_ge(s_gath[0][1], 16 * TILES * HALF + 16)
                    dve.wait_ge(s_edge[1], 16 * HALF + 16)
                    dve.tensor_tensor(msg[0:TAIL, 1, 0, 0:D], gath[0:TAIL, 1, 0, :],
                                      edg[0:TAIL, 1, 0, :], ALU.mult).then_inc(s_msg, 1)
                add_window(GROUPS, 1, r, rows)
                dve.wait_ge(s_add[r], GROUPS + 1 + SLOTS)
                leftover_dve(dve, r, rows)
                if r == 0:
                    between_dve(dve)
            final_dve(dve)

        def between_pe(pe, product):
            pe.wait_ge(s_w, 8 * 16)

            def first_layer(c, s):
                pe.wait_ge(s_x1, c + 1)
                pe.wait_ge(s_y1, c + 1)
                pe.matmul(bigA[0:D, s, :], w1[:], sumT[0][0:D, nodes_of(c)], start=True, stop=True
                          ).then_inc(s_y1mm, 1)

            def second_layer(c, s):
                pe.wait_ge(s_zx, c + 1)
                for t in range(CT):
                    tr = pe.transpose(bigC[:, t * (D + 1):(t + 1) * (D + 1)],
                                      sumT[0][:, tile_nodes(c, t)], ident[0:D + 1, 0:D + 1])
                tr.then_inc(s_x1n, 1)
                pe.wait_ge(s_y1, c + 1 + SLOTS)
                product(c, bigB[:, s], lambda t: y1[:, s, t * P:(t + 1) * P], w2, s_y2, c + 1, s_y2mm)

            written_out(first_layer, second_layer)

            def turn(c, s):
                pe.wait_ge(s_x2, c + 1)
                pe.wait_ge(s_x2T, c + 1)
                for t in range(CT):
                    tr = pe.transpose(bigA[0:D, s, t * P:(t + 1) * P],
                                      nat[:, bass.ds(c * CT + t, 1), :].rearrange("p a d -> p (a d)"),
                                      ident[:])
                tr.then_inc(s_x2t, 1)

            def linears(c, s):
                pe.wait_ge(s_x2T, c + 1 + SLOTS)
                product(c, bigB[:, s], lambda t: featT[:, tile_nodes(c, t)], w_lin, s_t, c + 1, s_tmm)
                product(c, bigC, lambda t: featT[:, tile_nodes(c, t)], w_root, s_root, c + 1, s_rmm)

            written_out(turn, linears)

        @block.tensor
        def _(pe):
            pe.wait_ge(s_x, 16)
            pe.wait_ge(s_wpre, 32)
            pe.wait_ge(s_init, 1)

            def product(c, bank, left_T, w, free, free_at, done):
                pe.wait_ge(free, free_at)
                for t in range(CT):
                    mm = pe.matmul(bank[:, t * D:(t + 1) * D], left_T(t), w[:], start=True, stop=True)
                mm.then_inc(done, 1)

            def pre(c, s):
                product(c, bigB[:, s], lambda t: featT[:, tile_nodes(c, t)], w_pre, s_h, c + 1, s_hmm)

            written_out(None, pre)

            pe.wait_ge(s_ext, 2)
            pe.wait_ge(s_const, 3)
            pe.transpose(bigC[0:1, 0:P], extent[:, 2:3], ident[:])
            pe.transpose(bigC[0:1, P:2 * P], extent[:, 3:4], ident[:]).then_inc(s_extT, 1)

            pe.sem_inc(s_seg[0], SLOTS)
            pe.sem_inc(s_seg[1], SLOTS)
            pe.sem_inc(s_y2mm, SLOTS)

            for r in range(2):
                rows = (D + 1, D)[r]
                values = (msg, gath)[r]

                def seg_sum(k, tiles, s, rows=rows, values=values):
                    for j in range(tiles):
                        mm = pe.matmul(seg[0:rows, s, 0:WIN], values[0:k, s, j, 0:rows],
                                       onehot[0:k, s, j, :], start=(j == 0), stop=(j == tiles - 1))
                    return mm

                def group(g, s, r=r):
                    pe.wait_ge(s_oh[r], g + 1)
                    if r == 0:
                        pe.wait_ge(s_msg, g + 1 + SLOTS)
                    else:
                        pe.wait_ge(s_gath[1][s], (g - s) * (8 * TILES) + 16 * TILES)
                    pe.wait_ge(s_add[r], g + 1)
                    seg_sum(P, TILES, s).then_inc(s_seg[r], 1)

                pairs(pe, GROUPS, group)
                pe.wait_ge(s_oh[r], GROUPS + 1)
                if r == 0:
                    pe.wait_ge(s_msg, GROUPS + 1 + SLOTS)
                else:
                    pe.wait_ge(s_gath[1][1], 16 * TILES * HALF + 16)
                pe.wait_ge(s_add[r], GROUPS + 1)
                seg_sum(TAIL, 1, 1).then_inc(s_seg[r], 1)

                with pe.If_ne(left_flag(pe, r), 0):
                    def left_group(g, k, tiles, r=r):
                        with pe.Fori(0, WINDOWS) as w:
                            if r == 0:
                                pe.wait_ge(s_lmsg, g + 2)
                            else:
                                pe.wait_ge(s_lgath[1], g * (16 * TILES) + 16 * tiles)
                            pe.wait_ge(s_loh[r], g * WINDOWS + w + 1)
                            pe.wait_ge(s_ladd[r], g * WINDOWS + w + 1)
                            seg_sum(k, tiles, 0).then_inc(s_lseg[r], 1)

                    with pe.Fori(0, GROUPS) as g:
                        left_group(g, P, TILES)
                    left_group(GROUPS, TAIL, 1)

                if r == 0:
                    between_pe(pe, product)

            pe.wait_ge(s_add[1], GROUPS + 1 + SLOTS)
            with pe.If_ne(left_flag(pe, 2), 0):
                pe.wait_ge(s_ladd[1], (GROUPS + 1) * WINDOWS + 1)

            def agg_nat(c, s):
                pe.wait_ge(s_f1, c + 1)
                for t in range(CT):
                    tr = pe.transpose(bigB[:, s, t * D:(t + 1) * D], sumT[1][:, tile_nodes(c, t)],
                                      ident[0:D, 0:D])
                tr.then_inc(s_aggn, 1)

            written_out(None, agg_nat)


def kernel(**inputs):
    import numpy as np
    import concourse.bacc as bacc
    from concourse.bass_utils import run_bass_kernel_spmd

    a = {k: np.asarray(v) for k, v in inputs.items()}

    def edge_columns(e):
        body = e[:GROUPS * GROUP].reshape(GROUPS, P, TILES).transpose(1, 0, 2).reshape(P, GROUPS * TILES)
        return body, e[GROUPS * GROUP:].reshape(TAIL, 1)

    src_body, src_tail = edge_columns(a["src"])
    dst_body, dst_tail = edge_columns(a["dst"])
    arrays = {
        "x": a["x"], "xT": a["x"].T,
        "src_body": src_body, "src_tail": src_tail, "dst_body": dst_body, "dst_tail": dst_tail,
        "first": a["dst"][::GROUP],
        "edge": a["edge_attr_96"],
        "W_pre": a["L0_gnn_W_pre"], "b_pre": a["L0_gnn_b_pre"].reshape(1, D),
        "W1": a["L0_gnn_W1"], "b1": a["L0_gnn_b1"].reshape(D, 1),
        "W2": a["L0_gnn_W2"], "b2": a["L0_gnn_b2"].reshape(1, D),
        "WlinT": a["L1_gnn_W_lin"].T, "b_lin": a["L1_gnn_b_lin"].reshape(1, D),
        "WrootT": a["L1_gnn_W_root"].T, "b_root": a["L1_gnn_b_root"].reshape(1, D),
    }
    arrays = {k: np.ascontiguousarray(v) for k, v in arrays.items()}
    nc = bacc.Bacc("TRN2", target_bir_lowering=False, num_devices=1)
    d = {k: nc.dram_tensor(f"in_{k}", v.shape, mybir.dt.from_np(v.dtype), kind="ExternalInput").ap()
         for k, v in arrays.items()}
    out = nc.dram_tensor("out_y", (N_NODES, D), F32, kind="ExternalOutput").ap()
    build(nc, d["x"], d["xT"], (d["src_body"], d["src_tail"]), (d["dst_body"], d["dst_tail"]),
          d["first"], d["edge"], d["W_pre"], d["b_pre"], d["W1"], d["b1"], d["W2"], d["b2"],
          d["WlinT"], d["b_lin"], d["WrootT"], d["b_root"], out)
    r = run_bass_kernel_spmd(nc, [{f"in_{k}": v for k, v in arrays.items()}], core_ids=[0])
    return r.results[0]["out_y"]
```

```python
from contextlib import ExitStack

import concourse.bass as bass
from concourse import mybir

F32 = mybir.dt.float32
I32 = mybir.dt.int32
ALU = mybir.AluOpType
ACT = mybir.ActivationFunctionType
AX = mybir.AxisListType

P = 128
N_NODES, D = 6250, 96
N_EDGES = 106250
EPS = 1e-5
SLOTS = 2

WIN = 128
WINDOWS = -(-N_NODES // WIN)
TILES = 10
GROUP = P * TILES
GROUPS = N_EDGES // GROUP
TAIL = N_EDGES - GROUPS * GROUP
COLS = GROUPS * TILES + 1

CT = 4
CN = CT * P
NT = -(-N_NODES // P)
NP = NT * P
CHUNKS = -(-NT // CT)
REST = N_NODES - (NT - 1) * P

PERIOD = N_EDGES * CN // N_NODES // GROUP + 1
LATE = 2
PAIRS = (CHUNKS - LATE - 1) // 2
LAST_RUN = PERIOD * (2 * PAIRS + 1)

assert 0 < TAIL <= P and NT == (CHUNKS - 1) * CT + 1 and CHUNKS % 2 == 1
assert PERIOD == 7 and GROUPS == LAST_RUN + PERIOD - 1


def build(nc, x, xT_in, src, dst, first, edge, W_pre, b_pre, W1, b1, W2, b2,
          WlinT, b_lin, WrootT, b_root, out):
    with ExitStack() as ctx:
        def sb(name, shape, dt=F32):
            return ctx.enter_context(nc.sbuf_tensor(name, shape, dt))

        def sem(name):
            return ctx.enter_context(nc.semaphore(name))

        def sems(name):
            return [sem(name + "_r0"), sem(name + "_r1")]

        table = [nc.dram_tensor("table_h", (NP, D), F32).ap(),
                 nc.dram_tensor("table_t", (NP, D), F32).ap()]

        xT = sb("xT", [D + 1, NP])
        sumT = [sb("sumT0", [D + 1, NP + WIN]),
                sb("sumT1", [D, NP + WIN])]
        x2 = sb("x2", [P, NT, D])
        root = sb("root", [P, NT, D])
        dinv = sb("dinv", [P, NT])
        srcs = sb("srcs", [P, COLS], I32)
        dsts = sb("dsts", [P, COLS], I32)
        base = sb("base", [P, GROUPS + 1], I32)
        rel = sb("rel", [P, COLS])
        ident = sb("ident", [P, P])
        iota = sb("iota", [P, WIN])
        win_start = sb("win_start", [P, WINDOWS])
        w_pre = sb("w_pre", [D + 1, D])
        w1 = sb("w1", [D, D])
        b1c = sb("b1c", [D, 1])
        w2 = sb("w2", [D + 1, D])
        w_lin = sb("w_lin", [D + 1, D])
        w_root = sb("w_root", [D + 1, D])

        slot_idx = sb("slot_idx", [P, SLOTS, TILES], I32)
        gath = sb("gath", [P, SLOTS, TILES, D])
        edg = sb("edg", [P, SLOTS, TILES, D])
        msg = sb("msg", [P, SLOTS, TILES, D + 1])
        onehot = sb("onehot", [P, SLOTS, TILES, WIN])

        colsT = sb("colsT", [D + 1, SLOTS, CN])
        xc = sb("xc", [P, SLOTS, CT, D])
        y1 = sb("y1", [D + 1, SLOTS, CN])
        y2 = sb("y2", [P, SLOTS, CT, D])
        z = sb("z", [P, SLOTS, CT, D])
        x2c = sb("x2c", [P, SLOTS, CT, D])
        x2T = sb("x2T", [D + 1, SLOTS, CN])
        ship = sb("ship", [P, SLOTS, CT, D])
        bns = sb("bns", [P, SLOTS, CT, 6])
        mean = sb("mean", [P, SLOTS, CT])
        gap = sb("gap", [P, SLOTS, CT])
        gap_sq = sb("gap_sq", [P, SLOTS, CT])
        spread = sb("spread", [P, SLOTS, 2, CT])
        inv = sb("inv", [P, SLOTS, 2, CT])

        left = sb("left", [P, COLS])
        left_t = sb("left_t", [P, COLS])
        left_w = sb("left_w", [P, TILES])
        extent = sb("extent", [P, 6])
        worst = sb("worst", [1, 1])
        flag = sb("flag", [1, 1], I32)

        segs = ctx.enter_context(nc.psum_tensor("segs", [P, SLOTS, 512], F32))
        bankA = ctx.enter_context(nc.psum_tensor("bankA", [P, SLOTS, 512], F32))
        bankB = ctx.enter_context(nc.psum_tensor("bankB", [P, SLOTS, 512], F32))
        bankC = ctx.enter_context(nc.psum_tensor("bankC", [P, SLOTS, 512], F32))
        seg = segs[:, :, 0:WIN]
        iota_ps = segs[:, 0, 512 - WIN:512]

        s_pad = sem("s_pad")
        s_ones = sem("s_ones")
        s_init = sem("s_init")
        s_identz = sem("s_identz")
        s_const = sem("s_const")
        s_zero = sem("s_zero")
        s_xT = [sem(f"s_xT{q}") for q in range(4)]
        s_wpre = sem("s_wpre")
        s_idx_in = sem("s_idx_in")
        s_w = sem("s_w")
        s_rel = sem("s_rel")
        s_ext = sem("s_ext")
        s_extT = sem("s_extT")
        s_flag = sem("s_flag")
        s_hmm = sem("s_hmm")
        s_h = sem("s_h")
        s_tab = sems("s_tab")
        s_slot = sems("s_slot")
        s_gath = [[sem(f"s_gath{r}_{s}") for s in range(SLOTS)] for r in range(2)]
        s_edge = [sem(f"s_edge{s}") for s in range(SLOTS)]
        s_go = sem("s_go")
        s_msg = sem("s_msg")
        s_oh = sems("s_oh")
        s_seg = sems("s_seg")
        s_add = sems("s_add")
        s_left = sem("s_left")
        s_lidx = sems("s_lidx")
        s_lgath = sems("s_lgath")
        s_ledge = sem("s_ledge")
        s_lmsg = sem("s_lmsg")
        s_lrel = sems("s_lrel")
        s_loh = sems("s_loh")
        s_lseg = sems("s_lseg")
        s_ladd = sems("s_ladd")
        s_xc = [sem(f"s_xc{s}") for s in range(SLOTS)]
        s_x1 = sem("s_x1")
        s_y1mm = sem("s_y1mm")
        s_x1n = sem("s_x1n")
        s_y1 = sem("s_y1")
        s_y2mm = sem("s_y2mm")
        s_y2 = sem("s_y2")
        s_zx = sem("s_zx")
        s_z = sem("s_z")
        s_x2 = sem("s_x2")
        s_x2t = sem("s_x2t")
        s_x2T = sem("s_x2T")
        s_tmm = sem("s_tmm")
        s_rmm = sem("s_rmm")
        s_root = sem("s_root")
        s_t = sem("s_t")
        s_agg = sem("s_agg")
        s_aggn = sem("s_aggn")
        s_f1 = sem("s_f1")
        s_f2 = sem("s_f2")
        s_f3 = sem("s_f3")
        s_y = sem("s_y")
        s_out = sem("s_out")
        s_stat = sems("s_stat")
        s_mean = sems("s_mean")
        s_var = sems("s_var")
        s_sqrt = sems("s_sqrt")
        s_inv = sems("s_inv")
        s_shipped = sems("s_shipped")

        edge_g = edge[0:GROUPS * GROUP, :].rearrange("(g p j) d -> g p (j d)", p=P, j=TILES)
        edge_tail = edge[GROUPS * GROUP:N_EDGES, :]
        TAIL_SLOT = GROUPS % SLOTS
        IN_SLOT = GROUPS // SLOTS

        def go_round(eng, group, tail, step):
            with eng.Fori(0, PERIOD // 2) as i:
                group(2 * i, 0)
                group(2 * i + 1, 1)
            group(PERIOD - 1, (PERIOD - 1) % 2)
            with eng.Fori(0, PAIRS) as i:
                for odd in range(2):
                    for k in range(PERIOD):
                        at = PERIOD * (odd + 1) + k
                        group(i * (2 * PERIOD) + at, at % 2)
                        step(k, 2 * i + odd, 2 * i + odd, odd, CT)
            for k in range(PERIOD - 1):
                group(LAST_RUN + k, (LAST_RUN + k) % 2)
                step(k, 2 * PAIRS, 2 * PAIRS, 0, CT)
            tail()
            step(PERIOD - 1, 2 * PAIRS, 2 * PAIRS, 0, CT)
            for k in range(PERIOD):
                step(k, CHUNKS - 2, CHUNKS - 2, 1, CT)
                step(k, CHUNKS - 1, CHUNKS - 1, 0, 1)

        def again(eng, step):
            with eng.Fori(0, CHUNKS // 2) as i:
                for odd in range(2):
                    for k in range(PERIOD):
                        step(k, 2 * i + odd + CHUNKS, 2 * i + odd, (odd + CHUNKS) % 2, CT)
            for k in range(PERIOD):
                step(k, 2 * CHUNKS - 1, CHUNKS - 1, (2 * CHUNKS - 1) % 2, 1)

        def pairs(eng, count, body):
            with eng.Fori(0, count // 2) as i:
                body(2 * i, 0)
                body(2 * i + 1, 1)
            body(count - 1, 0)

        def nodes_of(c, tiles=CT):
            return bass.ds(c * CN, tiles * P)

        def tiles_of(c, tiles=CT):
            return bass.ds(c * CT, tiles)

        def flat(a):
            return a.rearrange("p t d -> p (t d)")

        def rows_of(tab, c, tiles):
            return tab[bass.ds(c * CN, tiles * P), :].rearrange("(t p) d -> p t d", p=P)

        def by_tile(bank, tiles, d=D):
            return bank[:, 0:tiles * d].rearrange("p (t d) -> p t d", d=d)

        def per_node(v, tiles):
            return v.unsqueeze(2).to_broadcast([P, tiles, D])

        def left_flag(eng):
            eng.wait_ge(s_flag, 1)
            reg = eng.alloc_register("left_flag")
            eng.reg_load(reg, flag[0:1, 0:1])
            return reg

        block = ctx.enter_context(nc.Block())

        @block.sync
        def _(sp):
            XQ = -(-CHUNKS // 4) * CN
            sp.wait_ge(s_pad, 1)
            for q in range(4):
                cols = slice(q * XQ, min((q + 1) * XQ, N_NODES))
                sp.dma_start(xT[0:D, cols], xT_in[:, cols]).then_inc(s_xT[q], 16)

            def store_h(c, tiles):
                sp.wait_ge(s_h, c + 1 + SLOTS)
                sp.dma_start(rows_of(table[0], c, tiles), root[:, tiles_of(c, tiles), :]
                             ).then_inc(s_tab[0], 16)

            with sp.Fori(0, CHUNKS - 1) as c:
                store_h(c, CT)
            store_h(CHUNKS - 1, 1)

            for dst_tile, src_ap in ((w1[:], W1), (b1c[:], b1),
                                     (w2[0:D, :], W2), (w2[D:D + 1, :], b2),
                                     (w_lin[0:D, :], WlinT), (w_lin[D:D + 1, :], b_lin),
                                     (w_root[0:D, :], WrootT), (w_root[D:D + 1, :], b_root)):
                sp.dma_start(dst_tile, src_ap).then_inc(s_w, 16)

            def load_edges(g, s):
                sp.dma_start(edg[:, s].rearrange("p j d -> p (j d)"),
                             edge_g[bass.ds(g, 1)].rearrange("g p f -> (g p) f")).then_inc(s_edge[s], 16)

            def load_tail():
                sp.dma_start(edg[0:TAIL, TAIL_SLOT, 0, :], edge_tail).then_inc(s_edge[TAIL_SLOT], 16)

            def group(g, s):
                if isinstance(g, int) and g == GROUPS - 1:
                    return
                sp.wait_ge(s_msg, g + 1 + SLOTS)
                if isinstance(g, int) and g == GROUPS - SLOTS:
                    load_tail()
                else:
                    load_edges(g + SLOTS, s)

            def step_0(k, n, c, s, tiles):
                if k == 0:
                    sp.wait_ge(s_zx, n + 1)
                    if tiles == CT:
                        sp.dma_start(xc[:, s], rows_of(x, c, CT)).then_inc(s_xc[s], 16)
                    else:
                        sp.dma_start(xc[0:REST, s, 0, :], x[N_NODES - REST:N_NODES, :]
                                     ).then_inc(s_xc[s], 16)
                if k == 6:
                    sp.wait_ge(s_t, n + 1 + SLOTS)
                    sp.dma_start(rows_of(table[1], c, tiles), ship[:, s, 0:tiles, :]
                                 ).then_inc(s_tab[1], 16)
                    sp.wait_ge(s_tab[1], n * 16 + 16)
                    sp.sem_inc(s_shipped[0], 1)

            def step_1(k, n, c, s, tiles):
                if k == 5:
                    sp.wait_ge(s_y, n + 1)
                    if tiles == CT:
                        sp.dma_start(rows_of(out, c, CT), ship[:, s]).then_inc(s_out, 16)
                    else:
                        sp.dma_start(out[N_NODES - REST:N_NODES, :], ship[0:REST, s, 0, :]
                                     ).then_inc(s_out, 16)
                    sp.wait_ge(s_out, n * 16 + 16)
                    sp.sem_inc(s_shipped[1], 1)

            sp.sem_inc(s_shipped[0], SLOTS)
            sp.sem_inc(s_shipped[1], SLOTS)
            flag_reg = left_flag(sp)
            for s in range(SLOTS):
                load_edges(s, s)
            go_round(sp, group, lambda: None, step_0)
            with sp.If_ne(flag_reg, 0):
                with sp.Fori(0, GROUPS) as g:
                    sp.wait_ge(s_lmsg, g + 1)
                    sp.dma_start(edg[:, 0].rearrange("p j d -> p (j d)"),
                                 edge_g[bass.ds(g, 1)].rearrange("g p f -> (g p) f")
                                 ).then_inc(s_ledge, 16)
                sp.wait_ge(s_lmsg, GROUPS + 1)
                sp.dma_start(edg[0:TAIL, 0, 0, :], edge_tail).then_inc(s_ledge, 16)
                again(sp, step_0)
            go_round(sp, lambda g, s: None, lambda: None, step_1)
            with sp.If_ne(flag_reg, 0):
                again(sp, step_1)
            sp.wait_ge(s_out, 16 * CHUNKS)

        @block.gpsimd
        def _(pool):
            pool.iota(iota[:], [[1, WIN]], base=0, channel_multiplier=0,
                      allow_small_or_imprecise_dtypes=True)
            pool.iota(win_start[:], [[WIN, WINDOWS]], base=0, channel_multiplier=0,
                      allow_small_or_imprecise_dtypes=True)
            taken_from = (PERIOD + 1) * TILES
            taken_step = PERIOD * TILES
            taken_last = taken_from + 2 * PAIRS * taken_step
            pool.memset(left[:, 0:taken_from], 0.0)
            pool.iota(left[:, taken_from:taken_last], [[CN, 2 * PAIRS], [0, taken_step]], base=CN,
                      channel_multiplier=0, allow_small_or_imprecise_dtypes=True)
            pool.memset(left[:, taken_last:COLS], float((2 * PAIRS + 1) * CN))
            pool.memset(ident[:], 0.0).then_inc(s_identz, 1)
            pool.wait_ge(s_identz, 1)
            pool.affine_select(out=ident[:], in_=ident[:], compare_op=ALU.not_equal, fill=1.0, base=0,
                               pattern=[[-1, P]], channel_multiplier=1).then_inc(s_const, 1)
            pool.memset(sumT[0][:], 0.0)
            pool.memset(sumT[1][:], 0.0).then_inc(s_zero, 1)
            flag_reg = left_flag(pool)

            for r in range(2):
                rows_used = (s_msg, s_seg[1])[r]

                def gather(g, s, r=r, rows_used=rows_used):
                    pool.wait_ge(rows_used, g + 1)
                    pool.wait_ge(s_slot[r], g + 1)
                    pool.sem_inc(s_go, 1)
                    for j in range(TILES):
                        pool.indirect_dma_start(
                            gath[:, s, j, :], None, table[r],
                            bass.IndirectOffsetOnAxis(ap=slot_idx[:, s, j:j + 1], axis=0)
                        ).then_inc(s_gath[r][s], 16)

                pool.wait_ge(s_tab[r], 16 * CHUNKS)
                if r == 1:
                    with pool.If_ne(flag_reg, 0):
                        pool.wait_ge(s_tab[1], 16 * 2 * CHUNKS)
                pairs(pool, GROUPS, gather)
                pool.wait_ge(rows_used, GROUPS + 1)
                pool.wait_ge(s_slot[r], GROUPS + 1)
                pool.indirect_dma_start(
                    gath[0:TAIL, TAIL_SLOT, 0, :], None, table[r],
                    bass.IndirectOffsetOnAxis(ap=slot_idx[0:TAIL, TAIL_SLOT, 0:1], axis=0)
                ).then_inc(s_gath[r][TAIL_SLOT], 16)

                with pool.If_ne(flag_reg, 0):
                    with pool.Fori(0, GROUPS) as g:
                        pool.wait_ge(s_lidx[r], g + 1)
                        pool.sem_inc(s_go, 1)
                        for j in range(TILES):
                            pool.indirect_dma_start(
                                gath[:, 0, j, :], None, table[r],
                                bass.IndirectOffsetOnAxis(ap=slot_idx[:, 0, j:j + 1], axis=0)
                            ).then_inc(s_lgath[r], 16)
                    pool.wait_ge(s_lidx[r], GROUPS + 1)
                    pool.indirect_dma_start(
                        gath[0:TAIL, 0, 0, :], None, table[r],
                        bass.IndirectOffsetOnAxis(ap=slot_idx[0:TAIL, 0, 0:1], axis=0)
                    ).then_inc(s_lgath[r], 16)

        @block.scalar
        def _(act):
            act.dma_start(w_pre[0:D, :], W_pre).then_inc(s_wpre, 16)
            act.dma_start(w_pre[D:D + 1, :], b_pre).then_inc(s_wpre, 16)
            act.dma_start(dsts[:, 0:COLS - 1], dst[0]).then_inc(s_idx_in, 16)
            act.dma_start(base[:], first.partition_broadcast(P)).then_inc(s_idx_in, 16)
            act.dma_start(srcs[:, 0:COLS - 1], src[0]).then_inc(s_idx_in, 16)
            act.wait_ge(s_pad, 2)
            act.dma_start(srcs[0:TAIL, COLS - 1:COLS], src[1]).then_inc(s_idx_in, 16)
            act.dma_start(dsts[0:TAIL, COLS - 1:COLS], dst[1]).then_inc(s_idx_in, 16)
            act.sem_inc(s_h, SLOTS)
            act.sem_inc(s_x2T, SLOTS)
            act.sem_inc(s_root, SLOTS)

            def gelu_h(c, s, tiles):
                act.wait_ge(s_hmm, c + 1)
                act.activation(flat(root[:, tiles_of(c, tiles), :]), bankB[:, s, 0:tiles * D], ACT.Gelu
                               ).then_inc(s_h, 1)

            with act.Fori(0, CHUNKS // 2) as i:
                gelu_h(2 * i, 0, CT)
                gelu_h(2 * i + 1, 1, CT)
            gelu_h(CHUNKS - 1, 0, 1)

            def step_0(k, n, c, s, tiles):
                if k == 1:
                    act.wait_ge(s_y1mm, n + 1)
                    act.activation(y1[0:D, s, 0:tiles * P], bankA[0:D, s, 0:tiles * P], ACT.Gelu,
                                   bias=b1c[:, 0:1]).then_inc(s_y1, 1)
                if k == 2:
                    act.wait_ge(s_y2mm, n + 1)
                    act.activation(flat(y2[:, s, 0:tiles]), bankB[:, s, 0:tiles * D], ACT.Gelu
                                   ).then_inc(s_y2, 1)
                if k == 3:
                    act.wait_ge(s_var[0], n + 1)
                    act.activation(spread[:, s, :, 0:tiles], spread[:, s, :, 0:tiles], ACT.Sqrt
                                   ).then_inc(s_sqrt[0], 1)
                if k == 4:
                    act.wait_ge(s_x2t, n + 1)
                    act.copy(x2T[0:D, s, 0:tiles * P], bankA[0:D, s, 0:tiles * P]).then_inc(s_x2T, 1)
                if k == 5:
                    act.copy(flat(x2[:, tiles_of(c, tiles), :]), flat(x2c[:, s, 0:tiles]))
                    act.wait_ge(s_rmm, n + 1)
                    act.copy(flat(root[:, tiles_of(c, tiles), :]), bankC[:, s, 0:tiles * D]
                             ).then_inc(s_root, 1)

            def step_1(k, n, c, s, tiles):
                if k == 3:
                    act.wait_ge(s_var[1], n + 1)
                    act.activation(spread[:, s, 0, 0:tiles], spread[:, s, 0, 0:tiles], ACT.Sqrt
                                   ).then_inc(s_sqrt[1], 1)

            act.wait_ge(s_idx_in, 5 * 16)
            flag_reg = left_flag(act)
            for r in range(2):
                def group(g, s, r=r):
                    if isinstance(g, int) and g == GROUPS - 1:
                        return
                    if r == 0:
                        act.wait_ge(s_gath[0][s], (g - s) * (8 * TILES) + 16 * TILES)
                    else:
                        act.wait_ge(s_gath[1][s], (g - s) * (8 * TILES) + 16 * TILES)
                    if isinstance(g, int) and g == GROUPS - SLOTS:
                        act.copy(slot_idx[0:TAIL, TAIL_SLOT, 0:1], srcs[0:TAIL, COLS - 1:COLS]
                                 ).then_inc(s_slot[r], 1)
                    else:
                        act.copy(slot_idx[:, s, :], srcs[:, bass.ds((g + SLOTS) * TILES, TILES)]
                                 ).then_inc(s_slot[r], 1)

                for s in range(SLOTS):
                    act.copy(slot_idx[:, s, :], srcs[:, s * TILES:(s + 1) * TILES]).then_inc(s_slot[r], 1)
                if r == 0:
                    act.wait_ge(s_w, 8 * 16)
                    act.wait_ge(s_tab[0], 16 * CHUNKS)
                go_round(act, group, lambda: None, (step_0, step_1)[r])

                with act.If_ne(flag_reg, 0):
                    with act.Fori(0, GROUPS) as g:
                        act.wait_ge(s_ladd[r], g * WINDOWS + 1)
                        act.copy(slot_idx[:, 0, :], srcs[:, bass.ds(g * TILES, TILES)]
                                 ).then_inc(s_lidx[r], 1)
                    act.wait_ge(s_ladd[r], GROUPS * WINDOWS + 1)
                    act.copy(slot_idx[0:TAIL, 0, 0:1], srcs[0:TAIL, COLS - 1:COLS]
                             ).then_inc(s_lidx[r], 1)
                    again(act, (step_0, step_1)[r])

        def leftover_dve(dve, r, rows):
            if r == 0:
                dve.tensor_scalar(left[:], rel[:], float(WIN), None, ALU.is_ge)
                dve.tensor_scalar(left_t[:], rel[:], 0.0, None, ALU.is_lt).then_inc(s_left, 1)
                dve.wait_ge(s_left, 1)
                dve.tensor_tensor(left[:], left[:], left_t[:], ALU.add).then_inc(s_left, 1)
                dve.wait_ge(s_left, 2)
                dve.tensor_scalar(left_t[:], dsts[:], 1.0, None, ALU.add).then_inc(s_left, 1)
                dve.wait_ge(s_left, 3)
                dve.tensor_tensor(left[:], left[:], left_t[:], ALU.mult).then_inc(s_left, 1)
                dve.wait_ge(s_left, 4)
                dve.tensor_scalar(left[:], left[:], -1.0, None, ALU.add).then_inc(s_left, 1)
                dve.wait_ge(s_left, 5)
                dve.sem_inc(s_lmsg, 1)
            dve.sem_inc(s_ladd[r], 1)

            def left_group(g, k, tiles):
                if r == 0:
                    dve.wait_ge(s_lgath[0], g * (16 * TILES) + 16 * tiles)
                    dve.wait_ge(s_ledge, g * 16 + 16)
                    dve.wait_ge(s_ladd[0], g * WINDOWS + 1)
                    dve.tensor_tensor(msg[0:k, 0, 0:tiles, 0:D], gath[0:k, 0, 0:tiles],
                                      edg[0:k, 0, 0:tiles], ALU.mult).then_inc(s_lmsg, 1)
                with dve.Fori(0, WINDOWS) as w:
                    dve.wait_ge(s_ladd[r], g * WINDOWS + w + 1)
                    dve.tensor_scalar(left_w[0:k, 0:tiles], left[0:k, bass.ds(g * TILES, tiles)],
                                      win_start[0:k, bass.ds(w, 1)], None, ALU.subtract
                                      ).then_inc(s_lrel[r], 1)
                    dve.wait_ge(s_lrel[r], g * WINDOWS + w + 1)
                    dve.tensor_tensor(
                        onehot[0:k, 0, 0:tiles],
                        iota_ps[0:k].unsqueeze(1).to_broadcast([k, tiles, WIN]),
                        left_w[0:k, 0:tiles].unsqueeze(2).to_broadcast([k, tiles, WIN]),
                        ALU.is_equal).then_inc(s_loh[r], 1)
                    dve.wait_ge(s_lseg[r], g * WINDOWS + w + 1)
                    dve.tensor_tensor(sumT[r][0:rows, bass.ds(w * WIN, WIN)],
                                      sumT[r][0:rows, bass.ds(w * WIN, WIN)],
                                      seg[0:rows, 0, :], ALU.add).then_inc(s_ladd[r], 1)

            with dve.Fori(0, GROUPS) as g:
                left_group(g, P, TILES)
            left_group(GROUPS, TAIL, 1)
            dve.wait_ge(s_ladd[r], (GROUPS + 1) * WINDOWS + 1)

        def mean_and_var(dve, r, n, s, tiles, ready):
            dve.wait_ge(ready, n + 1)
            for t in range(tiles):
                last = dve.bn_stats(bns[:, s, t, :], z[:, s, t, :])
            last.then_inc(s_stat[r], 1)
            dve.wait_ge(s_stat[r], n + 1)
            even, dev_even, odd, dev_odd = (bns[:, s, 0:tiles, q] for q in (1, 2, 4, 5))
            m, g, q, v = mean[:, s, 0:tiles], gap[:, s, 0:tiles], gap_sq[:, s, 0:tiles], \
                spread[:, s, 0, 0:tiles]
            dve.tensor_tensor(m, even, odd, ALU.add)
            dve.tensor_tensor(g, even, odd, ALU.subtract)
            dve.tensor_tensor(v, dev_even, dev_odd, ALU.add).then_inc(s_mean[r], 1)
            dve.wait_ge(s_mean[r], n * 2 + 1)
            dve.tensor_scalar(m, m, 0.5, None, ALU.mult)
            dve.scalar_tensor_tensor(out=q, in0=g, scalar=0.25, in1=g, op0=ALU.mult, op1=ALU.mult)
            dve.tensor_scalar(v, v, 1.0 / D, EPS, ALU.mult, ALU.add).then_inc(s_mean[r], 1)
            dve.wait_ge(s_mean[r], n * 2 + 2)
            dve.tensor_tensor(v, v, q, ALU.add).then_inc(s_var[r], 1)

        def normalise(dve, s, tiles, to):
            for t in range(tiles):
                last = dve.tensor_scalar(to[:, s, t, :], z[:, s, t, :], mean[:, s, t:t + 1],
                                         inv[:, s, 0, t:t + 1], ALU.subtract, ALU.mult)
            return last

        def node_stage_0(dve, k, n, c, s, tiles, added):
            if k == 0:
                dve.wait_ge(s_add[0], added + SLOTS)
                dve.tensor_tensor(colsT[:, s, 0:tiles * P], sumT[0][:, nodes_of(c, tiles)],
                                  xT[:, nodes_of(c, tiles)], ALU.add).then_inc(s_x1, 1)
            if k == 3:
                dve.wait_ge(s_x1n, n + 1)
                dve.wait_ge(s_xc[s], (n - s) * 8 + 16)
                turned = by_tile(bankC[:, s], tiles, D + 1)
                dve.tensor_scalar(spread[:, s, 1, 0:tiles], turned[:, :, D], -1.0, 1.0,
                                  ALU.add, ALU.max)
                dve.tensor_tensor(z[:, s, 0:tiles], xc[:, s, 0:tiles], turned[:, :, 0:D], ALU.add
                                  ).then_inc(s_zx, 1)
                dve.wait_ge(s_zx, n + 1 + SLOTS)
                dve.wait_ge(s_y2, n + 1)
                dve.tensor_tensor(z[:, s, 0:tiles], z[:, s, 0:tiles], y2[:, s, 0:tiles], ALU.add
                                  ).then_inc(s_z, 1)
                mean_and_var(dve, 0, n, s, tiles, s_z)
            if k == 4:
                dve.wait_ge(s_sqrt[0], n + 1)
                dve.reciprocal(inv[:, s, :, 0:tiles], spread[:, s, :, 0:tiles]).then_inc(s_inv[0], 1)
                dve.wait_ge(s_inv[0], n + 1)
                normalise(dve, s, tiles, x2c).then_inc(s_x2, 1)
                dve.tensor_copy(dinv[:, tiles_of(c, tiles)], inv[:, s, 1, 0:tiles])
            if k == 5:
                dve.wait_ge(s_tmm, n + 1)
                dve.wait_ge(s_shipped[0], n + 1)
                dve.tensor_tensor(ship[:, s, 0:tiles], by_tile(bankB[:, s], tiles),
                                  per_node(inv[:, s, 1, 0:tiles], tiles), ALU.mult).then_inc(s_t, 1)

        def node_stage_1(dve, k, n, c, s, tiles, added):
            if k == 0:
                dve.wait_ge(s_add[1], added + SLOTS)
                dve.tensor_copy(colsT[0:D, s, 0:tiles * P], sumT[1][:, nodes_of(c, tiles)]
                                ).then_inc(s_agg, 1)
            if k == 2:
                dve.wait_ge(s_aggn, n + 1)
                dve.tensor_tensor(z[:, s, 0:tiles], by_tile(bankB[:, s], tiles),
                                  per_node(dinv[:, tiles_of(c, tiles)], tiles), ALU.mult
                                  ).then_inc(s_f1, 1)
                dve.wait_ge(s_f1, n + 1 + SLOTS)
                dve.tensor_tensor(z[:, s, 0:tiles], z[:, s, 0:tiles], root[:, tiles_of(c, tiles), :],
                                  ALU.add).then_inc(s_f2, 1)
                dve.wait_ge(s_f2, n + 1)
                dve.scalar_tensor_tensor(out=flat(z[:, s, 0:tiles]), in0=flat(z[:, s, 0:tiles]),
                                         scalar=0.0, in1=flat(x2[:, tiles_of(c, tiles), :]),
                                         op0=ALU.max, op1=ALU.add).then_inc(s_f3, 1)
                mean_and_var(dve, 1, n, s, tiles, s_f3)
            if k == 4:
                dve.wait_ge(s_sqrt[1], n + 1)
                dve.reciprocal(inv[:, s, 0, 0:tiles], spread[:, s, 0, 0:tiles]).then_inc(s_inv[1], 1)
                dve.wait_ge(s_shipped[1], n + 1)
                dve.wait_ge(s_inv[1], n + 1)
                normalise(dve, s, tiles, ship).then_inc(s_y, 1)

        @block.vector
        def _(dve):
            dve.memset(xT[:, N_NODES:NP], 0.0).then_inc(s_pad, 1)
            dve.memset(srcs[:, COLS - 1:COLS], 0)
            dve.memset(dsts[:, COLS - 1:COLS], N_NODES - 1).then_inc(s_pad, 1)
            dve.wait_ge(s_pad, 1)
            dve.memset(xT[D:D + 1, :], 1.0).then_inc(s_ones, 1)
            dve.wait_ge(s_const, 1)
            dve.tensor_copy(iota_ps, iota[:])
            dve.memset(msg[:, :, :, D:D + 1], 1.0)
            dve.memset(y1[D:D + 1, :, :], 1.0)
            dve.memset(x2T[D:D + 1, :, :], 1.0).then_inc(s_init, 1)

            dve.wait_ge(s_idx_in, 5 * 16)
            dve.tensor_tensor(
                rel[:, 0:COLS - 1].rearrange("p (g j) -> p g j", j=TILES),
                dsts[:, 0:COLS - 1].rearrange("p (g j) -> p g j", j=TILES),
                base[:, 0:GROUPS].unsqueeze(2).to_broadcast([P, GROUPS, TILES]),
                ALU.subtract)
            dve.memset(rel[:, COLS - 1:COLS], 0.0).then_inc(s_rel, 1)
            dve.wait_ge(s_rel, 1)
            dve.tensor_tensor(rel[0:TAIL, COLS - 1:COLS], dsts[0:TAIL, COLS - 1:COLS],
                              base[0:TAIL, GROUPS:GROUPS + 1], ALU.subtract)
            dve.tensor_tensor(left_t[:], dsts[:], left[:], ALU.subtract).then_inc(s_rel, 1)
            dve.wait_ge(s_rel, 2)
            dve.tensor_reduce(extent[:, 0:1], rel[:], AX.X, ALU.max)
            dve.tensor_reduce(extent[:, 1:2], rel[:], AX.X, ALU.min)
            dve.tensor_reduce(extent[:, 2:3], left_t[:], AX.X, ALU.min).then_inc(s_ext, 1)
            dve.wait_ge(s_ext, 1)
            dve.tensor_scalar(extent[:, 3:4], extent[:, 0:1], -float(WIN - 1), None, ALU.add)
            dve.tensor_scalar(extent[:, 4:6], extent[:, 1:3], -1.0, None, ALU.mult).then_inc(s_ext, 1)
            dve.wait_ge(s_extT, 1)
            dve.tensor_reduce(worst[:], bankC[0:1, 0, 0:3 * P], AX.X, ALU.max).then_inc(s_ext, 1)
            dve.wait_ge(s_ext, 3)
            dve.tensor_scalar(flag[:], worst[:], 0.0, None, ALU.is_gt).then_inc(s_flag, 1)

            for credited in (s_msg, s_add[0], s_add[1], s_zx, s_t, s_f1):
                dve.sem_inc(credited, SLOTS)
            flag_reg = left_flag(dve)
            dve.wait_ge(s_zero, 1)
            dve.wait_ge(s_init, 1)

            for r in range(2):
                rows = (D + 1, D)[r]

                def add_window(g, s, r=r, rows=rows):
                    b = dve.value_load(base[0:1, bass.ds(g, 1)], min_val=0, max_val=N_NODES - 1)
                    dve.wait_ge(s_seg[r], g + 1 + SLOTS)
                    dve.wait_ge(s_add[r], g + SLOTS)
                    dve.tensor_tensor(sumT[r][0:rows, bass.ds(b, WIN)], sumT[r][0:rows, bass.ds(b, WIN)],
                                      seg[0:rows, s, :], ALU.add).then_inc(s_add[r], 1)

                def group(g, s, r=r):
                    dve.wait_ge(s_seg[r], g + 1)
                    dve.tensor_tensor(
                        onehot[:, s], iota_ps.unsqueeze(1).to_broadcast([P, TILES, WIN]),
                        rel[:, bass.ds(g * TILES, TILES)].unsqueeze(2).to_broadcast([P, TILES, WIN]),
                        ALU.is_equal).then_inc(s_oh[r], 1)
                    if r == 0:
                        dve.wait_ge(s_gath[0][s], (g - s) * (8 * TILES) + 16 * TILES)
                        dve.wait_ge(s_edge[s], (g - s) * 8 + 16)
                        dve.tensor_tensor(msg[:, s, :, 0:D], gath[:, s], edg[:, s], ALU.mult
                                          ).then_inc(s_msg, 1)
                    add_window(g, s)

                def tail(r=r):
                    s = TAIL_SLOT
                    dve.wait_ge(s_seg[r], GROUPS + 1)
                    dve.tensor_tensor(onehot[0:TAIL, s, 0, :], iota_ps[0:TAIL, :],
                                      rel[0:TAIL, COLS - 1:COLS].to_broadcast([TAIL, WIN]),
                                      ALU.is_equal).then_inc(s_oh[r], 1)
                    if r == 0:
                        dve.wait_ge(s_gath[0][s], 16 * TILES * IN_SLOT + 16)
                        dve.wait_ge(s_edge[s], 16 * IN_SLOT + 16)
                        dve.tensor_tensor(msg[0:TAIL, s, 0, 0:D], gath[0:TAIL, s, 0, :],
                                          edg[0:TAIL, s, 0, :], ALU.mult).then_inc(s_msg, 1)
                    add_window(GROUPS, s)

                def step(k, n, c, s, tiles, r=r):
                    late = isinstance(c, int) and c >= CHUNKS - LATE
                    added = GROUPS + 1 if late else c * PERIOD + PERIOD + 1
                    (node_stage_0, node_stage_1)[r](dve, k, n, c, s, tiles, added)

                def step_again(k, n, c, s, tiles, r=r):
                    (node_stage_0, node_stage_1)[r](dve, k, n, c, s, tiles, GROUPS + 1)

                if r == 1:
                    dve.wait_ge(s_root, CHUNKS + SLOTS)
                go_round(dve, group, tail, step)
                with dve.If_ne(flag_reg, 0):
                    leftover_dve(dve, r, rows)
                    again(dve, step_again)
                    if r == 0:
                        dve.wait_ge(s_root, 2 * CHUNKS + SLOTS)

        @block.tensor
        def _(pe):
            pe.wait_ge(s_wpre, 32)
            pe.wait_ge(s_ones, 1)

            def product(bank, left_T, w, tiles):
                for t in range(tiles):
                    last = pe.matmul(bank[:, t * D:(t + 1) * D], left_T[:, t * P:(t + 1) * P], w[:],
                                     start=True, stop=True)
                return last

            for c in range(CHUNKS):
                tiles = CT if c < CHUNKS - 1 else 1
                if c % 4 == 0:
                    pe.wait_ge(s_xT[c // 4], 16)
                pe.wait_ge(s_h, c + 1)
                product(bankB[:, c % 2], xT[:, c * CN:c * CN + tiles * P], w_pre, tiles
                        ).then_inc(s_hmm, 1)

            pe.wait_ge(s_ext, 2)
            pe.wait_ge(s_const, 1)
            for q in range(3):
                last = pe.transpose(bankC[0:1, 0, q * P:(q + 1) * P], extent[:, 3 + q:4 + q], ident[:])
            last.then_inc(s_extT, 1)

            pe.sem_inc(s_seg[0], SLOTS)
            pe.sem_inc(s_seg[1], SLOTS)
            flag_reg = left_flag(pe)
            pe.wait_ge(s_w, 8 * 16)
            pe.wait_ge(s_init, 1)

            def step_0(k, n, c, s, tiles):
                if k == 1:
                    pe.wait_ge(s_x1, n + 1)
                    pe.wait_ge(s_x2T, n + 1)
                    pe.matmul(bankA[0:D, s, 0:tiles * P], w1[:], colsT[0:D, s, 0:tiles * P],
                              start=True, stop=True).then_inc(s_y1mm, 1)
                    pe.wait_ge(s_root, n + 1)
                    for t in range(tiles):
                        last = pe.transpose(bankC[:, s, t * (D + 1):(t + 1) * (D + 1)],
                                            colsT[:, s, t * P:(t + 1) * P], ident[0:D + 1, 0:D + 1])
                    last.then_inc(s_x1n, 1)
                if k == 2:
                    pe.wait_ge(s_y1, n + 1)
                    pe.wait_ge(s_t, n + 1)
                    product(bankB[:, s], y1[:, s], w2, tiles).then_inc(s_y2mm, 1)
                if k == 4:
                    pe.wait_ge(s_x2, n + 1)
                    for t in range(tiles):
                        last = pe.transpose(bankA[0:D, s, t * P:(t + 1) * P], x2c[:, s, t, :], ident[:])
                    last.then_inc(s_x2t, 1)
                if k == 5:
                    pe.wait_ge(s_x2T, n + 1 + SLOTS)
                    product(bankB[:, s], x2T[:, s], w_lin, tiles).then_inc(s_tmm, 1)
                    product(bankC[:, s], x2T[:, s], w_root, tiles).then_inc(s_rmm, 1)

            def step_1(k, n, c, s, tiles):
                if k == 1:
                    pe.wait_ge(s_agg, n + 1)
                    pe.wait_ge(s_f1, n + 1)
                    for t in range(tiles):
                        last = pe.transpose(bankB[:, s, t * D:(t + 1) * D],
                                            colsT[0:D, s, t * P:(t + 1) * P], ident[0:D, 0:D])
                    last.then_inc(s_aggn, 1)

            for r in range(2):
                rows = (D + 1, D)[r]
                values = (msg, gath)[r]

                def seg_sum(k, tiles, s, rows=rows, values=values):
                    for j in range(tiles):
                        last = pe.matmul(seg[0:rows, s, :], values[0:k, s, j, 0:rows],
                                         onehot[0:k, s, j, :], start=(j == 0), stop=(j == tiles - 1))
                    return last

                def group(g, s, r=r, seg_sum=seg_sum):
                    pe.wait_ge(s_oh[r], g + 1)
                    if r == 0:
                        pe.wait_ge(s_msg, g + 1 + SLOTS)
                    else:
                        pe.wait_ge(s_gath[1][s], (g - s) * (8 * TILES) + 16 * TILES)
                    pe.wait_ge(s_add[r], g + 1)
                    seg_sum(P, TILES, s).then_inc(s_seg[r], 1)

                def tail(r=r, seg_sum=seg_sum):
                    pe.wait_ge(s_oh[r], GROUPS + 1)
                    if r == 0:
                        pe.wait_ge(s_msg, GROUPS + 1 + SLOTS)
                    else:
                        pe.wait_ge(s_gath[1][TAIL_SLOT], 16 * TILES * IN_SLOT + 16)
                    pe.wait_ge(s_add[r], GROUPS + 1)
                    seg_sum(TAIL, 1, TAIL_SLOT).then_inc(s_seg[r], 1)

                def left_group(g, k, tiles, r=r, seg_sum=seg_sum):
                    with pe.Fori(0, WINDOWS) as w:
                        if r == 0:
                            pe.wait_ge(s_lmsg, g + 2)
                        else:
                            pe.wait_ge(s_lgath[1], g * (16 * TILES) + 16 * tiles)
                        pe.wait_ge(s_loh[r], g * WINDOWS + w + 1)
                        pe.wait_ge(s_ladd[r], g * WINDOWS + w + 1)
                        seg_sum(k, tiles, 0).then_inc(s_lseg[r], 1)

                go_round(pe, group, tail, (step_0, step_1)[r])
                with pe.If_ne(flag_reg, 0):
                    with pe.Fori(0, GROUPS) as g:
                        left_group(g, P, TILES)
                    left_group(GROUPS, TAIL, 1)
                    again(pe, (step_0, step_1)[r])


def kernel(**inputs):
    import numpy as np
    import concourse.bacc as bacc
    from concourse.bass_utils import run_bass_kernel_spmd

    a = {k: np.asarray(v) for k, v in inputs.items()}

    def edge_columns(e):
        body = e[:GROUPS * GROUP].reshape(GROUPS, P, TILES).transpose(1, 0, 2).reshape(P, GROUPS * TILES)
        return body, e[GROUPS * GROUP:].reshape(TAIL, 1)

    src_body, src_tail = edge_columns(a["src"])
    dst_body, dst_tail = edge_columns(a["dst"])
    arrays = {
        "x": a["x"], "xT": a["x"].T,
        "src_body": src_body, "src_tail": src_tail, "dst_body": dst_body, "dst_tail": dst_tail,
        "first": a["dst"][::GROUP],
        "edge": a["edge_attr_96"],
        "W_pre": a["L0_gnn_W_pre"], "b_pre": a["L0_gnn_b_pre"].reshape(1, D),
        "W1": a["L0_gnn_W1"], "b1": a["L0_gnn_b1"].reshape(D, 1),
        "W2": a["L0_gnn_W2"], "b2": a["L0_gnn_b2"].reshape(1, D),
        "WlinT": a["L1_gnn_W_lin"].T, "b_lin": a["L1_gnn_b_lin"].reshape(1, D),
        "WrootT": a["L1_gnn_W_root"].T, "b_root": a["L1_gnn_b_root"].reshape(1, D),
    }
    arrays = {k: np.ascontiguousarray(v) for k, v in arrays.items()}
    nc = bacc.Bacc("TRN2", target_bir_lowering=False, num_devices=1)
    d = {k: nc.dram_tensor(f"in_{k}", v.shape, mybir.dt.from_np(v.dtype), kind="ExternalInput").ap()
         for k, v in arrays.items()}
    out = nc.dram_tensor("out_y", (N_NODES, D), F32, kind="ExternalOutput").ap()
    build(nc, d["x"], d["xT"], (d["src_body"], d["src_tail"]), (d["dst_body"], d["dst_tail"]),
          d["first"], d["edge"], d["W_pre"], d["b_pre"], d["W1"], d["b1"], d["W2"], d["b2"],
          d["WlinT"], d["b_lin"], d["WrootT"], d["b_root"], out)
    r = run_bass_kernel_spmd(nc, [{f"in_{k}": v for k, v in arrays.items()}], core_ids=[0])
    return r.results[0]["out_y"]
```

```python
from contextlib import ExitStack

import concourse.bass as bass
from concourse import mybir

F32 = mybir.dt.float32
I32 = mybir.dt.int32
ALU = mybir.AluOpType
ACT = mybir.ActivationFunctionType
AX = mybir.AxisListType

P = 128
N_NODES, D = 6250, 96
N_EDGES = 106250
EPS = 1e-5
SLOTS = 2

WIN = 128
WINDOWS = -(-N_NODES // WIN)
TILES = 10
GROUP = P * TILES
GROUPS = N_EDGES // GROUP
TAIL = N_EDGES - GROUPS * GROUP
COLS = GROUPS * TILES + 1

CT = 4
CN = CT * P
NT = -(-N_NODES // P)
NP = NT * P
CHUNKS = -(-NT // CT)
REST = N_NODES - (NT - 1) * P

PERIOD = N_EDGES * CN // N_NODES // GROUP + 1
PAIRS = (CHUNKS - 3) // 2
LAST_RUN = PERIOD * (2 * PAIRS + 1)
LAST_STEPS = ((0,), (1, 2), (3,), (4,), (5, 6))
AHEAD = ((2, 3), (PERIOD, PERIOD))
EARLY = 3
EARLY_TILES = EARLY * TILES
BATCHES = -(-EARLY_TILES // CT)
XT_AT = (0, 1, 4, 8, CHUNKS)
PARTS = ((0, 5), (5, 8), (8, TILES))
HALF = TILES // 2

assert 0 < TAIL <= P and NT == (CHUNKS - 1) * CT + 1 and CHUNKS % 2 == 1
assert EARLY + 2 * SLOTS <= PERIOD
assert PERIOD == 7 and GROUPS == LAST_RUN + len(LAST_STEPS) + 1
assert HALF * D <= 512 and all(b <= HALF or a >= HALF for a, b in PARTS)


def build(nc, x, xT_in, src, dst, first, edge, W_pre, b_pre, W1, b1, W2, b2,
          WlinT, b_lin, WrootT, b_root, out):
    with ExitStack() as ctx:
        def sb(name, shape, dt=F32):
            return ctx.enter_context(nc.sbuf_tensor(name, shape, dt))

        def sem(name):
            return ctx.enter_context(nc.semaphore(name))

        def sems(name):
            return [sem(name + "_r0"), sem(name + "_r1")]

        table = [nc.dram_tensor("table_h", (NP, D), F32).ap(),
                 nc.dram_tensor("table_t", (NP, D), F32).ap()]

        xT = sb("xT", [D + 1, NP])
        sumT = [sb("sumT0", [D + 1, NP + WIN]),
                sb("sumT1", [D, NP + WIN])]
        x2 = sb("x2", [P, NT, D])
        root = sb("root", [P, NT, D])
        dinv = sb("dinv", [P, NT])
        srcs = sb("srcs", [P, COLS], I32)
        dsts = sb("dsts", [P, COLS], I32)
        base = sb("base", [P, GROUPS + 1], I32)
        rel = sb("rel", [P, COLS])
        ident = sb("ident", [P, P])
        iota = sb("iota", [P, WIN])
        win_start = sb("win_start", [P, WINDOWS])
        w_pre = sb("w_pre", [D + 1, D])
        w1 = sb("w1", [D, D])
        b1c = sb("b1c", [D, 1])
        w2 = sb("w2", [D + 1, D])
        w_lin = sb("w_lin", [D + 1, D])
        w_root = sb("w_root", [D + 1, D])

        slot_idx = sb("slot_idx", [P, SLOTS, TILES], I32)
        gath = sb("gath", [P, SLOTS, TILES, D])
        edg = sb("edg", [P, SLOTS, TILES, D])
        msg = sb("msg", [P, SLOTS, TILES, D + 1])
        onehot = sb("onehot", [P, SLOTS, TILES, WIN])

        colsT = sb("colsT", [D + 1, SLOTS, CN])
        xc = sb("xc", [P, SLOTS, CT, D])
        y1 = sb("y1", [D + 1, SLOTS, CN])
        y2 = sb("y2", [P, SLOTS, CT, D])
        z = sb("z", [P, SLOTS, CT, D])
        x2c = sb("x2c", [P, SLOTS, CT, D])
        x2T = sb("x2T", [D + 1, SLOTS, CN])
        ship = sb("ship", [P, SLOTS, CT, D])
        bns = sb("bns", [P, SLOTS, CT, 6])
        mean = sb("mean", [P, SLOTS, CT])
        gap = sb("gap", [P, SLOTS, CT])
        gap_sq = sb("gap_sq", [P, SLOTS, CT])
        spread = sb("spread", [P, SLOTS, 2, CT])
        inv = sb("inv", [P, SLOTS, 2, CT])

        left = sb("left", [P, COLS])
        left_t = sb("left_t", [P, COLS])
        left_w = sb("left_w", [P, TILES])
        extent = sb("extent", [P, 6])
        worst = sb("worst", [1, 1])
        flag = sb("flag", [1, 1], I32)

        def bank(name, shape):
            return ctx.enter_context(nc.psum_tensor(name, shape, F32))

        segs = bank("segs", [P, SLOTS, 512])
        bank_a, bank_b, bank_c = (bank(f"bank_{q}", [P, 512]) for q in "abc")
        bank_d = bank("bank_d", [P, 512])
        edg_ps = bank("edg_ps", [P, 2, 512])
        seg = segs[:, :, 0:WIN]
        area_a = (bank_a, segs[:, 0, WIN:2 * WIN])
        area_b = (bank_b, segs[:, 1, WIN:WIN + P])
        area_c = (bank_c, bank_d[:, 0:P])
        iota_ps = bank_d[:, 512 - WIN:512]

        s_pad = sem("s_pad")
        s_ones = sem("s_ones")
        s_init = sem("s_init")
        s_identz = sem("s_identz")
        s_const = sem("s_const")
        s_zero = sem("s_zero")
        s_xT = [sem(f"s_xT{q}") for q in range(4)]
        s_wpre = sem("s_wpre")
        s_src_early = sem("s_src_early")
        s_idx_in = sem("s_idx_in")
        s_w = sem("s_w")
        s_rel = sem("s_rel")
        s_ext = sem("s_ext")
        s_extT = sem("s_extT")
        s_flag = sem("s_flag")
        s_hmm = sem("s_hmm")
        s_h = sem("s_h")
        s_tab = sems("s_tab")
        s_xrows = [sem(f"s_xrows{b}") for b in range(BATCHES)]
        s_xrows_turned = sem("s_xrows_turned")
        s_xrows_kept = sem("s_xrows_kept")
        s_slot = sems("s_slot")
        s_gath = [[sem(f"s_gath{r}_{s}") for s in range(SLOTS)] for r in range(2)]
        s_edge = [sem(f"s_edge{s}") for s in range(SLOTS)]
        s_edge_ps = sem("s_edge_ps")
        s_part = [[sem(f"s_part{r}_{q}") for q in range(len(PARTS))] for r in range(2)]
        s_msg_part = sem("s_msg_part")
        s_go = sem("s_go")
        s_msg = sem("s_msg")
        s_oh = sems("s_oh")
        s_seg = sems("s_seg")
        s_add = sems("s_add")
        s_left = sem("s_left")
        s_lidx = sems("s_lidx")
        s_lgath = sems("s_lgath")
        s_ledge = sem("s_ledge")
        s_lmsg = sem("s_lmsg")
        s_lrel = sems("s_lrel")
        s_loh = sems("s_loh")
        s_lseg = sems("s_lseg")
        s_ladd = sems("s_ladd")
        s_xc = [sem(f"s_xc{s}") for s in range(SLOTS)]
        s_x1 = sem("s_x1")
        s_y1mm = sem("s_y1mm")
        s_x1n = sem("s_x1n")
        s_y1 = sem("s_y1")
        s_y2mm = sem("s_y2mm")
        s_y2 = sem("s_y2")
        s_zx = sem("s_zx")
        s_z = sem("s_z")
        s_x2 = sem("s_x2")
        s_x2t = sem("s_x2t")
        s_x2T = sem("s_x2T")
        s_tmm = sem("s_tmm")
        s_rmm = sem("s_rmm")
        s_root = sem("s_root")
        s_t = sem("s_t")
        s_agg = sem("s_agg")
        s_aggn = sem("s_aggn")
        s_f1 = sem("s_f1")
        s_f2 = sem("s_f2")
        s_f3 = sem("s_f3")
        s_y = sem("s_y")
        s_out = sem("s_out")
        s_stat = sems("s_stat")
        s_mean = sems("s_mean")
        s_var = sems("s_var")
        s_sqrt = sems("s_sqrt")
        s_inv = sems("s_inv")
        s_shipped = sems("s_shipped")

        edge_g = edge[0:GROUPS * GROUP, :].rearrange("(g p j) d -> g p (j d)", p=P, j=TILES)
        edge_tail = edge[GROUPS * GROUP:N_EDGES, :]
        TAIL_SLOT = GROUPS % SLOTS
        IN_SLOT = GROUPS // SLOTS

        def go_round(eng, group, tail, step, ahead):
            for g in range(PERIOD):
                group(g, g % 2)
            with eng.Fori(0, PAIRS) as i:
                for odd in range(2):
                    for k in range(PERIOD):
                        at = PERIOD * (odd + 1) + k
                        group(i * (2 * PERIOD) + at, at % 2)
                        step(k, 2 * i + odd, 2 * i + odd, odd, CT)
            for i, steps in enumerate(LAST_STEPS):
                group(LAST_RUN + i, (LAST_RUN + i) % 2)
                for k in steps:
                    step(k, CHUNKS - 3, CHUNKS - 3, 0, CT)
            before_group, before_tail = ahead
            for k in range(before_group):
                step(k, CHUNKS - 2, CHUNKS - 2, 1, CT)
            group(GROUPS - 1, (GROUPS - 1) % 2)
            for k in range(before_group, before_tail):
                step(k, CHUNKS - 2, CHUNKS - 2, 1, CT)
            tail()
            for k in range(PERIOD):
                if k >= before_tail:
                    step(k, CHUNKS - 2, CHUNKS - 2, 1, CT)
                step(k, CHUNKS - 1, CHUNKS - 1, 0, 1)

        def again(eng, step):
            with eng.Fori(0, CHUNKS // 2) as i:
                for odd in range(2):
                    for k in range(PERIOD):
                        step(k, 2 * i + odd + CHUNKS, 2 * i + odd, (odd + CHUNKS) % 2, CT)
            for k in range(PERIOD):
                step(k, 2 * CHUNKS - 1, CHUNKS - 1, (2 * CHUNKS - 1) % 2, 1)

        def nodes_of(c, tiles=CT):
            return bass.ds(c * CN, tiles * P)

        def tiles_of(c, tiles=CT):
            return bass.ds(c * CT, tiles)

        def flat(a):
            return a.rearrange("p t d -> p (t d)")

        def rows_of(tab, c, tiles):
            return tab[bass.ds(c * CN, tiles * P), :].rearrange("(t p) d -> p t d", p=P)

        def by_tile(bank, tiles, d=D):
            return bank[:, 0:tiles * d].rearrange("p (t d) -> p t d", d=d)

        def per_node(v, tiles):
            return v.unsqueeze(2).to_broadcast([P, tiles, D])

        def landed(r, g, s):
            return (g - s) * (8 * TILES) + 16 * TILES * (1 - early_in_slot(r, s))

        def early_in_slot(r, s):
            return (EARLY - s + 1) // SLOTS if r == 0 else 0

        def batch(b):
            return range(b * CT, min((b + 1) * CT, EARLY_TILES))

        def early(r, g):
            return r == 0 and isinstance(g, int) and g < EARLY

        def left_flag(eng):
            eng.wait_ge(s_flag, 1)
            reg = eng.alloc_register("left_flag")
            eng.reg_load(reg, flag[0:1, 0:1])
            return reg

        block = ctx.enter_context(nc.Block())

        @block.sync
        def _(sp):
            sp.dma_start(w_pre[0:D, :], W_pre).then_inc(s_wpre, 16)
            for q in range(4):
                cols = slice(XT_AT[q] * CN, min(XT_AT[q + 1] * CN, N_NODES))
                sp.dma_start(xT[0:D, cols], xT_in[:, cols]).then_inc(s_xT[q], 16)

            def load_edges(g, s):
                sp.dma_start(edg[:, s].rearrange("p j d -> p (j d)"),
                             edge_g[bass.ds(g, 1)].rearrange("g p f -> (g p) f")).then_inc(s_edge[s], 16)

            for s in range(SLOTS):
                load_edges(s, s)

            def store_h(c, tiles):
                sp.wait_ge(s_h, c + 1 + SLOTS)
                sp.dma_start(rows_of(table[0], c, tiles), root[:, tiles_of(c, tiles), :]
                             ).then_inc(s_tab[0], 16)

            with sp.Fori(0, CHUNKS - 1) as c:
                store_h(c, CT)
            store_h(CHUNKS - 1, 1)

            for dst_tile, src_ap in ((w1[:], W1), (b1c[:], b1),
                                     (w2[0:D, :], W2), (w2[D:D + 1, :], b2),
                                     (w_lin[0:D, :], WlinT), (w_lin[D:D + 1, :], b_lin),
                                     (w_root[0:D, :], WrootT), (w_root[D:D + 1, :], b_root)):
                sp.dma_start(dst_tile, src_ap).then_inc(s_w, 16)

            def load_tail():
                sp.dma_start(edg[0:TAIL, TAIL_SLOT, 0, :], edge_tail).then_inc(s_edge[TAIL_SLOT], 16)

            def group(g, s):
                if isinstance(g, int) and g == GROUPS - 1:
                    return
                sp.wait_ge(s_edge_ps, g + 1)
                if isinstance(g, int) and g == GROUPS - SLOTS:
                    load_tail()
                else:
                    load_edges(g + SLOTS, s)

            def step_0(k, n, c, s, tiles):
                if k == 0:
                    sp.wait_ge(s_zx, n + 1)
                    if tiles == CT:
                        sp.dma_start(xc[:, s], rows_of(x, c, CT)).then_inc(s_xc[s], 16)
                    else:
                        sp.dma_start(xc[0:REST, s, 0, :], x[N_NODES - REST:N_NODES, :]
                                     ).then_inc(s_xc[s], 16)
                if k == 6:
                    sp.wait_ge(s_t, n + 1 + SLOTS)
                    sp.dma_start(rows_of(table[1], c, tiles), ship[:, s, 0:tiles, :]
                                 ).then_inc(s_tab[1], 16)
                    if isinstance(n, int) and n == CHUNKS - 2:
                        return
                    sp.wait_ge(s_tab[1], n * 16 + 16)
                    sp.sem_inc(s_shipped[0], 2 if isinstance(n, int) and n == CHUNKS - 1 else 1)

            def step_1(k, n, c, s, tiles):
                if k == 5:
                    sp.wait_ge(s_y, n + 1)
                    if tiles == CT:
                        sp.dma_start(rows_of(out, c, CT), ship[:, s]).then_inc(s_out, 16)
                    else:
                        sp.dma_start(out[N_NODES - REST:N_NODES, :], ship[0:REST, s, 0, :]
                                     ).then_inc(s_out, 16)
                    sp.wait_ge(s_out, n * 16 + 16)
                    sp.sem_inc(s_shipped[1], 1)

            sp.sem_inc(s_shipped[0], SLOTS)
            sp.sem_inc(s_shipped[1], SLOTS)
            flag_reg = left_flag(sp)
            go_round(sp, group, lambda: None, step_0, AHEAD[0])
            with sp.If_ne(flag_reg, 0):
                with sp.Fori(0, GROUPS) as g:
                    sp.wait_ge(s_lmsg, g + 1)
                    sp.dma_start(edg[:, 0].rearrange("p j d -> p (j d)"),
                                 edge_g[bass.ds(g, 1)].rearrange("g p f -> (g p) f")
                                 ).then_inc(s_ledge, 16)
                sp.wait_ge(s_lmsg, GROUPS + 1)
                sp.dma_start(edg[0:TAIL, 0, 0, :], edge_tail).then_inc(s_ledge, 16)
                again(sp, step_0)
            go_round(sp, lambda g, s: None, lambda: None, step_1, AHEAD[1])
            with sp.If_ne(flag_reg, 0):
                again(sp, step_1)
            sp.wait_ge(s_out, 16 * CHUNKS)

        @block.gpsimd
        def _(pool):
            pool.iota(iota[:], [[1, WIN]], base=0, channel_multiplier=0,
                      allow_small_or_imprecise_dtypes=True)
            pool.iota(win_start[:], [[WIN, WINDOWS]], base=0, channel_multiplier=0,
                      allow_small_or_imprecise_dtypes=True)
            taken_from = (PERIOD + 1) * TILES
            taken_step = PERIOD * TILES
            taken_last = taken_from + 2 * PAIRS * taken_step
            pool.memset(left[:, 0:taken_from], 0.0)
            pool.iota(left[:, taken_from:taken_last], [[CN, 2 * PAIRS], [0, taken_step]], base=CN,
                      channel_multiplier=0, allow_small_or_imprecise_dtypes=True)
            pool.memset(left[:, taken_last:(GROUPS - 1) * TILES], float((CHUNKS - 2) * CN))
            pool.memset(left[:, (GROUPS - 1) * TILES:COLS], float((CHUNKS - 1) * CN))
            pool.memset(ident[:], 0.0).then_inc(s_identz, 1)
            pool.wait_ge(s_identz, 1)
            pool.affine_select(out=ident[:], in_=ident[:], compare_op=ALU.not_equal, fill=1.0, base=0,
                               pattern=[[-1, P]], channel_multiplier=1).then_inc(s_const, 1)

            pool.wait_ge(s_src_early, 16)
            for t in range(EARLY_TILES):
                pool.indirect_dma_start(
                    x2[:, t, :], None, x, bass.IndirectOffsetOnAxis(ap=srcs[:, t:t + 1], axis=0)
                ).then_inc(s_xrows[t // CT], 16)
            flag_reg = left_flag(pool)

            for r in range(2):
                rows_used = (s_msg, s_seg[1])[r]

                skipped = (EARLY, 0)[r]

                def gather(g, s, r=r, rows_used=rows_used, skipped=skipped):
                    if not isinstance(g, int) or g >= skipped + SLOTS:
                        pool.wait_ge(rows_used, g + 1)
                    pool.wait_ge(s_slot[r], g + 1 - skipped)
                    pool.sem_inc(s_go, 1)
                    for j in range(TILES):
                        pool.indirect_dma_start(
                            gath[:, s, j, :], None, table[r],
                            bass.IndirectOffsetOnAxis(ap=slot_idx[:, s, j:j + 1], axis=0)
                        ).then_inc(s_gath[r][s], 16)

                pool.wait_ge(s_tab[r], 16 * CHUNKS)
                if r == 1:
                    with pool.If_ne(flag_reg, 0):
                        pool.wait_ge(s_tab[1], 16 * 2 * CHUNKS)
                looped = (skipped + SLOTS + 1) // 2
                for g in range(skipped, 2 * looped):
                    gather(g, g % SLOTS)
                with pool.Fori(looped, GROUPS // 2) as i:
                    gather(2 * i, 0)
                    gather(2 * i + 1, 1)
                pool.wait_ge(rows_used, GROUPS)
                pool.wait_ge(s_slot[r], GROUPS - skipped)
                for q, (a, b) in enumerate(PARTS):
                    for j in range(a, b):
                        pool.indirect_dma_start(
                            gath[:, 0, j, :], None, table[r],
                            bass.IndirectOffsetOnAxis(ap=slot_idx[:, 0, j:j + 1], axis=0)
                        ).then_inc(s_part[r][q], 16)
                pool.wait_ge(rows_used, GROUPS + 1)
                pool.wait_ge(s_slot[r], GROUPS + 1 - skipped)
                pool.indirect_dma_start(
                    gath[0:TAIL, TAIL_SLOT, 0, :], None, table[r],
                    bass.IndirectOffsetOnAxis(ap=slot_idx[0:TAIL, TAIL_SLOT, 0:1], axis=0)
                ).then_inc(s_gath[r][TAIL_SLOT], 16)

                with pool.If_ne(flag_reg, 0):
                    with pool.Fori(0, GROUPS) as g:
                        pool.wait_ge(s_lidx[r], g + 1)
                        pool.sem_inc(s_go, 1)
                        for j in range(TILES):
                            pool.indirect_dma_start(
                                gath[:, 0, j, :], None, table[r],
                                bass.IndirectOffsetOnAxis(ap=slot_idx[:, 0, j:j + 1], axis=0)
                            ).then_inc(s_lgath[r], 16)
                    pool.wait_ge(s_lidx[r], GROUPS + 1)
                    pool.indirect_dma_start(
                        gath[0:TAIL, 0, 0, :], None, table[r],
                        bass.IndirectOffsetOnAxis(ap=slot_idx[0:TAIL, 0, 0:1], axis=0)
                    ).then_inc(s_lgath[r], 16)

        @block.scalar
        def _(act):
            act.dma_start(srcs[:, 0:EARLY_TILES], src[0][:, 0:EARLY_TILES]).then_inc(s_src_early, 16)
            act.dma_start(w_pre[D:D + 1, :], b_pre).then_inc(s_wpre, 16)
            act.dma_start(dsts[:, 0:COLS - 1], dst[0]).then_inc(s_idx_in, 16)
            act.dma_start(base[:], first.partition_broadcast(P)).then_inc(s_idx_in, 16)
            act.dma_start(srcs[:, EARLY_TILES:COLS - 1], src[0][:, EARLY_TILES:]).then_inc(s_idx_in, 16)
            act.wait_ge(s_pad, 1)
            act.dma_start(srcs[0:TAIL, COLS - 1:COLS], src[1]).then_inc(s_idx_in, 16)
            act.dma_start(dsts[0:TAIL, COLS - 1:COLS], dst[1]).then_inc(s_idx_in, 16)
            act.sem_inc(s_h, SLOTS)
            act.sem_inc(s_x2T, SLOTS)
            act.sem_inc(s_root, SLOTS)

            for c in range(CHUNKS):
                tiles = CT if c < CHUNKS - 1 else 1
                act.wait_ge(s_hmm, c + 1)
                act.activation(flat(root[:, tiles_of(c, tiles), :]), (bank_b, bank_c)[c % 2][:, 0:tiles * D],
                               ACT.Gelu).then_inc(s_h, 1)

            def first_slots(r, g):
                for first in range(g, g + SLOTS):
                    act.copy(slot_idx[:, first % SLOTS, :], srcs[:, first * TILES:(first + 1) * TILES]
                             ).then_inc(s_slot[r], 1)

            act.wait_ge(s_idx_in, 5 * 16)
            first_slots(0, EARLY)

            def edges_to_psum(g, s):
                act.wait_ge(s_edge[s], (g - s) * 8 + 16)
                act.copy(edg_ps[:, :, 0:HALF * D], edg[:, s].rearrange("p (h j) d -> p h (j d)", h=2)
                         ).then_inc(s_edge_ps, 1)

            edges_to_psum(0, 0)

            act.wait_ge(s_init, 1)
            for b in range(BATCHES + 1):
                if b < BATCHES:
                    act.wait_ge(s_xrows_turned, b + 1)
                    cols = slice(0, len(batch(b)) * P)
                    act.copy(x2T[0:D, b % SLOTS, cols], bank_a[0:D, cols]).then_inc(s_xrows_kept, 1)
                if b > 0:
                    c = CHUNKS + b - 1
                    act.wait_ge(s_hmm, c + 1)
                    tiles = batch(b - 1)
                    act.activation(flat(x2[:, tiles.start:tiles.stop, :]),
                                   (bank_b, bank_c)[c % 2][:, 0:len(tiles) * D], ACT.Gelu
                                   ).then_inc(s_h, 1)

            def step_0(k, n, c, s, tiles):
                if k == 1:
                    act.wait_ge(s_y1mm, n + 1)
                    act.activation(y1[0:D, s, 0:tiles * P], area_a[tiles == 1][0:D, 0:tiles * P], ACT.Gelu,
                                   bias=b1c[:, 0:1]).then_inc(s_y1, 1)
                if k == 2:
                    act.wait_ge(s_y2mm, n + 1)
                    act.activation(flat(y2[:, s, 0:tiles]), area_b[tiles == 1][:, 0:tiles * D], ACT.Gelu
                                   ).then_inc(s_y2, 1)
                if k == 3:
                    act.wait_ge(s_var[0], n + 1)
                    act.activation(spread[:, s, :, 0:tiles], spread[:, s, :, 0:tiles], ACT.Sqrt
                                   ).then_inc(s_sqrt[0], 1)
                if k == 4:
                    act.wait_ge(s_x2t, n + 1)
                    act.copy(x2T[0:D, s, 0:tiles * P], area_a[tiles == 1][0:D, 0:tiles * P]).then_inc(s_x2T, 1)
                if k == 6:
                    act.copy(flat(x2[:, tiles_of(c, tiles), :]), flat(x2c[:, s, 0:tiles]))
                    act.wait_ge(s_rmm, n + 1)
                    act.copy(flat(root[:, tiles_of(c, tiles), :]), area_c[tiles == 1][:, 0:tiles * D]
                             ).then_inc(s_root, 1)

            def step_1(k, n, c, s, tiles):
                if k == 3:
                    act.wait_ge(s_var[1], n + 1)
                    act.activation(spread[:, s, 0, 0:tiles], spread[:, s, 0, 0:tiles], ACT.Sqrt
                                   ).then_inc(s_sqrt[1], 1)

            flag_reg = left_flag(act)
            for r in range(2):
                def group(g, s, r=r):
                    if not (early(r, g) or isinstance(g, int) and g == GROUPS - 1):
                        act.wait_ge(s_gath[r][s], landed(r, g, s))
                        if isinstance(g, int) and g == GROUPS - SLOTS:
                            act.copy(slot_idx[0:TAIL, TAIL_SLOT, 0:1], srcs[0:TAIL, COLS - 1:COLS]
                                     ).then_inc(s_slot[r], 1)
                        else:
                            act.copy(slot_idx[:, s, :], srcs[:, bass.ds((g + SLOTS) * TILES, TILES)]
                                     ).then_inc(s_slot[r], 1)
                    if r == 0:
                        act.wait_ge(s_msg, g + 1 + SLOTS)
                        if isinstance(g, int) and g == GROUPS - 1:
                            act.wait_ge(s_edge[TAIL_SLOT], 16 * IN_SLOT + 16)
                            act.copy(edg_ps[0:TAIL, 0, 0:D], edg[0:TAIL, TAIL_SLOT, 0, :]
                                     ).then_inc(s_edge_ps, 1)
                        else:
                            edges_to_psum(g + 1, 1 - s)

                if r == 1:
                    first_slots(1, 0)
                else:
                    act.wait_ge(s_w, 8 * 16)
                    act.wait_ge(s_tab[0], 16 * CHUNKS)
                go_round(act, group, lambda: None, (step_0, step_1)[r], AHEAD[r])

                with act.If_ne(flag_reg, 0):
                    with act.Fori(0, GROUPS) as g:
                        act.wait_ge(s_ladd[r], g * WINDOWS + 1)
                        act.copy(slot_idx[:, 0, :], srcs[:, bass.ds(g * TILES, TILES)]
                                 ).then_inc(s_lidx[r], 1)
                    act.wait_ge(s_ladd[r], GROUPS * WINDOWS + 1)
                    act.copy(slot_idx[0:TAIL, 0, 0:1], srcs[0:TAIL, COLS - 1:COLS]
                             ).then_inc(s_lidx[r], 1)
                    again(act, (step_0, step_1)[r])

        def leftover_dve(dve, r, rows):
            if r == 0:
                dve.tensor_scalar(left[:], rel[:], float(WIN), None, ALU.is_ge)
                dve.tensor_scalar(left_t[:], rel[:], 0.0, None, ALU.is_lt).then_inc(s_left, 1)
                dve.wait_ge(s_left, 1)
                dve.tensor_tensor(left[:], left[:], left_t[:], ALU.add).then_inc(s_left, 1)
                dve.wait_ge(s_left, 2)
                dve.tensor_scalar(left_t[:], dsts[:], 1.0, None, ALU.add).then_inc(s_left, 1)
                dve.wait_ge(s_left, 3)
                dve.tensor_tensor(left[:], left[:], left_t[:], ALU.mult).then_inc(s_left, 1)
                dve.wait_ge(s_left, 4)
                dve.tensor_scalar(left[:], left[:], -1.0, None, ALU.add).then_inc(s_left, 1)
                dve.wait_ge(s_left, 5)
                dve.sem_inc(s_lmsg, 1)
            dve.sem_inc(s_ladd[r], 1)

            def left_group(g, k, tiles):
                if r == 0:
                    dve.wait_ge(s_lgath[0], g * (16 * TILES) + 16 * tiles)
                    dve.wait_ge(s_ledge, g * 16 + 16)
                    dve.wait_ge(s_ladd[0], g * WINDOWS + 1)
                    dve.tensor_tensor(msg[0:k, 0, 0:tiles, 0:D], gath[0:k, 0, 0:tiles],
                                      edg[0:k, 0, 0:tiles], ALU.mult).then_inc(s_lmsg, 1)
                with dve.Fori(0, WINDOWS) as w:
                    dve.wait_ge(s_ladd[r], g * WINDOWS + w + 1)
                    dve.tensor_scalar(left_w[0:k, 0:tiles], left[0:k, bass.ds(g * TILES, tiles)],
                                      win_start[0:k, bass.ds(w, 1)], None, ALU.subtract
                                      ).then_inc(s_lrel[r], 1)
                    dve.wait_ge(s_lrel[r], g * WINDOWS + w + 1)
                    dve.tensor_tensor(
                        onehot[0:k, 0, 0:tiles],
                        iota_ps[0:k].unsqueeze(1).to_broadcast([k, tiles, WIN]),
                        left_w[0:k, 0:tiles].unsqueeze(2).to_broadcast([k, tiles, WIN]),
                        ALU.is_equal).then_inc(s_loh[r], 1)
                    dve.wait_ge(s_lseg[r], g * WINDOWS + w + 1)
                    dve.tensor_tensor(sumT[r][0:rows, bass.ds(w * WIN, WIN)],
                                      sumT[r][0:rows, bass.ds(w * WIN, WIN)],
                                      seg[0:rows, 0, :], ALU.add).then_inc(s_ladd[r], 1)

            with dve.Fori(0, GROUPS) as g:
                left_group(g, P, TILES)
            left_group(GROUPS, TAIL, 1)
            dve.wait_ge(s_ladd[r], (GROUPS + 1) * WINDOWS + 1)

        def mean_and_var(dve, r, n, s, tiles, ready):
            dve.wait_ge(ready, n + 1)
            for t in range(tiles):
                last = dve.bn_stats(bns[:, s, t, :], z[:, s, t, :])
            last.then_inc(s_stat[r], 1)
            dve.wait_ge(s_stat[r], n + 1)
            even, dev_even, odd, dev_odd = (bns[:, s, 0:tiles, q] for q in (1, 2, 4, 5))
            m, g, q, v = mean[:, s, 0:tiles], gap[:, s, 0:tiles], gap_sq[:, s, 0:tiles], \
                spread[:, s, 0, 0:tiles]
            dve.tensor_tensor(m, even, odd, ALU.add)
            dve.tensor_tensor(g, even, odd, ALU.subtract)
            dve.tensor_tensor(v, dev_even, dev_odd, ALU.add).then_inc(s_mean[r], 1)
            dve.wait_ge(s_mean[r], n * 2 + 1)
            dve.tensor_scalar(m, m, 0.5, None, ALU.mult)
            dve.scalar_tensor_tensor(out=q, in0=g, scalar=0.25, in1=g, op0=ALU.mult, op1=ALU.mult)
            dve.tensor_scalar(v, v, 1.0 / D, EPS, ALU.mult, ALU.add).then_inc(s_mean[r], 1)
            dve.wait_ge(s_mean[r], n * 2 + 2)
            dve.tensor_tensor(v, v, q, ALU.add).then_inc(s_var[r], 1)

        def normalise(dve, s, tiles, to):
            for t in range(tiles):
                last = dve.tensor_scalar(to[:, s, t, :], z[:, s, t, :], mean[:, s, t:t + 1],
                                         inv[:, s, 0, t:t + 1], ALU.subtract, ALU.mult)
            return last

        def node_stage_0(dve, k, n, c, s, tiles, added):
            if k == 0:
                dve.wait_ge(s_add[0], added + SLOTS)
                dve.tensor_tensor(colsT[:, s, 0:tiles * P], sumT[0][:, nodes_of(c, tiles)],
                                  xT[:, nodes_of(c, tiles)], ALU.add).then_inc(s_x1, 1)
            if k == 3:
                dve.wait_ge(s_x1n, n + 1)
                dve.wait_ge(s_xc[s], (n - s) * 8 + 16)
                turned = by_tile(area_c[tiles == 1], tiles, D + 1)
                dve.tensor_scalar(spread[:, s, 1, 0:tiles], turned[:, :, D], -1.0, 1.0,
                                  ALU.add, ALU.max)
                dve.tensor_tensor(z[:, s, 0:tiles], xc[:, s, 0:tiles], turned[:, :, 0:D], ALU.add
                                  ).then_inc(s_zx, 1)
                dve.wait_ge(s_zx, n + 1 + SLOTS)
                dve.wait_ge(s_y2, n + 1)
                dve.tensor_tensor(z[:, s, 0:tiles], z[:, s, 0:tiles], y2[:, s, 0:tiles], ALU.add
                                  ).then_inc(s_z, 1)
                mean_and_var(dve, 0, n, s, tiles, s_z)
            if k == 4:
                dve.wait_ge(s_sqrt[0], n + 1)
                dve.reciprocal(inv[:, s, :, 0:tiles], spread[:, s, :, 0:tiles]).then_inc(s_inv[0], 1)
                dve.wait_ge(s_inv[0], n + 1)
                normalise(dve, s, tiles, x2c).then_inc(s_x2, 1)
                dve.tensor_copy(dinv[:, tiles_of(c, tiles)], inv[:, s, 1, 0:tiles])
            if k == 5:
                dve.wait_ge(s_tmm, n + 1)
                dve.wait_ge(s_shipped[0], n + 1)
                dve.tensor_tensor(ship[:, s, 0:tiles], by_tile(area_b[tiles == 1], tiles),
                                  per_node(inv[:, s, 1, 0:tiles], tiles), ALU.mult).then_inc(s_t, 1)

        def node_stage_1(dve, k, n, c, s, tiles, added):
            if k == 0:
                dve.wait_ge(s_add[1], added + SLOTS)
                dve.tensor_copy(colsT[0:D, s, 0:tiles * P], sumT[1][:, nodes_of(c, tiles)]
                                ).then_inc(s_agg, 1)
            if k == 2:
                dve.wait_ge(s_aggn, n + 1)
                dve.tensor_tensor(z[:, s, 0:tiles], by_tile(area_b[tiles == 1], tiles),
                                  per_node(dinv[:, tiles_of(c, tiles)], tiles), ALU.mult
                                  ).then_inc(s_f1, 1)
                dve.wait_ge(s_f1, n + 1 + SLOTS)
                dve.tensor_tensor(z[:, s, 0:tiles], z[:, s, 0:tiles], root[:, tiles_of(c, tiles), :],
                                  ALU.add).then_inc(s_f2, 1)
                dve.wait_ge(s_f2, n + 1)
                dve.scalar_tensor_tensor(out=flat(z[:, s, 0:tiles]), in0=flat(z[:, s, 0:tiles]),
                                         scalar=0.0, in1=flat(x2[:, tiles_of(c, tiles), :]),
                                         op0=ALU.max, op1=ALU.add).then_inc(s_f3, 1)
                mean_and_var(dve, 1, n, s, tiles, s_f3)
            if k == 4:
                dve.wait_ge(s_sqrt[1], n + 1)
                dve.reciprocal(inv[:, s, 0, 0:tiles], spread[:, s, 0, 0:tiles]).then_inc(s_inv[1], 1)
                dve.wait_ge(s_shipped[1], n + 1)
                dve.wait_ge(s_inv[1], n + 1)
                normalise(dve, s, tiles, ship).then_inc(s_y, 1)

        @block.vector
        def _(dve):
            dve.memset(srcs[:, COLS - 1:COLS], 0)
            dve.memset(dsts[:, COLS - 1:COLS], N_NODES - 1)
            dve.memset(xT[:, N_NODES:NP], 0.0).then_inc(s_pad, 1)
            dve.wait_ge(s_pad, 1)
            for q in range(4):
                dve.memset(xT[D:D + 1, XT_AT[q] * CN:min(XT_AT[q + 1] * CN, NP)], 1.0).then_inc(s_ones, 1)
            dve.wait_ge(s_const, 1)
            dve.tensor_copy(iota_ps, iota[:])
            dve.memset(msg[:, :, :, D:D + 1], 1.0)
            dve.memset(y1[D:D + 1, :, :], 1.0)
            dve.memset(x2T[D:D + 1, :, :], 1.0).then_inc(s_init, 1)

            dve.wait_ge(s_idx_in, 5 * 16)
            dve.tensor_tensor(
                rel[:, 0:COLS - 1].rearrange("p (g j) -> p g j", j=TILES),
                dsts[:, 0:COLS - 1].rearrange("p (g j) -> p g j", j=TILES),
                base[:, 0:GROUPS].unsqueeze(2).to_broadcast([P, GROUPS, TILES]),
                ALU.subtract)
            dve.memset(rel[:, COLS - 1:COLS], 0.0).then_inc(s_rel, 1)
            dve.wait_ge(s_rel, 1)
            dve.tensor_tensor(rel[0:TAIL, COLS - 1:COLS], dsts[0:TAIL, COLS - 1:COLS],
                              base[0:TAIL, GROUPS:GROUPS + 1], ALU.subtract)
            dve.tensor_tensor(left_t[:], dsts[:], left[:], ALU.subtract).then_inc(s_rel, 1)
            dve.wait_ge(s_rel, 2)
            dve.tensor_reduce(extent[:, 0:1], rel[:], AX.X, ALU.max)
            dve.tensor_reduce(extent[:, 1:2], rel[:], AX.X, ALU.min)
            dve.tensor_reduce(extent[:, 2:3], left_t[:], AX.X, ALU.min).then_inc(s_ext, 1)
            dve.wait_ge(s_ext, 1)
            dve.tensor_scalar(extent[:, 3:4], extent[:, 0:1], -float(WIN - 1), None, ALU.add)
            dve.tensor_scalar(extent[:, 4:6], extent[:, 1:3], -1.0, None, ALU.mult).then_inc(s_ext, 1)
            dve.memset(sumT[0][:], 0.0).then_inc(s_zero, 1)
            dve.wait_ge(s_extT, 1)
            dve.tensor_reduce(worst[:], bank_a[0:1, 0:3 * P], AX.X, ALU.max).then_inc(s_ext, 1)
            dve.wait_ge(s_ext, 3)
            dve.tensor_scalar(flag[:], worst[:], 0.0, None, ALU.is_gt).then_inc(s_flag, 1)
            dve.memset(sumT[1][:], 0.0).then_inc(s_zero, 1)

            for credited in (s_msg, s_add[0], s_add[1], s_zx, s_t, s_f1):
                dve.sem_inc(credited, SLOTS)
            flag_reg = left_flag(dve)
            dve.wait_ge(s_zero, 2)
            dve.wait_ge(s_init, 1)

            def edge_tiles(a, b):
                first_tile = a - a // HALF * HALF
                return edg_ps[:, a // HALF, first_tile * D:(first_tile + b - a) * D].rearrange(
                    "p (j d) -> p j d", d=D)

            for r in range(2):
                rows = (D + 1, D)[r]

                def add_window(g, s, r=r, rows=rows):
                    b = dve.value_load(base[0:1, bass.ds(g, 1)], min_val=0, max_val=N_NODES - 1)
                    dve.wait_ge(s_seg[r], g + 1 + SLOTS)
                    dve.wait_ge(s_add[r], g + SLOTS)
                    dve.tensor_tensor(sumT[r][0:rows, bass.ds(b, WIN)], sumT[r][0:rows, bass.ds(b, WIN)],
                                      seg[0:rows, s, :], ALU.add).then_inc(s_add[r], 1)

                def one_hots(g, s, r=r):
                    dve.wait_ge(s_seg[r], g + 1)
                    dve.tensor_tensor(
                        onehot[:, s], iota_ps.unsqueeze(1).to_broadcast([P, TILES, WIN]),
                        rel[:, bass.ds(g * TILES, TILES)].unsqueeze(2).to_broadcast([P, TILES, WIN]),
                        ALU.is_equal).then_inc(s_oh[r], 1)

                def group(g, s, r=r, one_hots=one_hots, add_window=add_window):
                    if not (r == 1 and isinstance(g, int) and g == GROUPS - 1):
                        one_hots(g, s)
                    if r == 0:
                        dve.wait_ge(s_edge_ps, g + 1)
                        if isinstance(g, int) and g == GROUPS - 1:
                            for q, (a, b) in enumerate(PARTS):
                                dve.wait_ge(s_part[0][q], 16 * (b - a))
                                dve.tensor_tensor(msg[:, s, a:b, 0:D], gath[:, s, a:b],
                                                  edge_tiles(a, b), ALU.mult
                                                  ).then_inc(s_msg if b == TILES else s_msg_part, 1)
                        else:
                            if early(0, g):
                                rows_h = x2[:, g * TILES:(g + 1) * TILES, :]
                                dve.wait_ge(s_h, CHUNKS - (-(g + 1) * TILES // CT) + SLOTS)
                            else:
                                rows_h = gath[:, s]
                                dve.wait_ge(s_gath[0][s], landed(0, g, s))
                            dve.tensor_tensor(
                                msg[:, s, :, 0:D].rearrange("p (h j) d -> p h j d", h=2),
                                rows_h.rearrange("p (h j) d -> p h j d", h=2),
                                edg_ps[:, :, 0:HALF * D].rearrange("p h (j d) -> p h j d", d=D),
                                ALU.mult).then_inc(s_msg, 1)
                    if isinstance(g, int) and 0 < g < PERIOD:
                        add_window(g - 1, 1 - s)
                    if not isinstance(g, int) or g >= PERIOD - 1:
                        add_window(g, s)
                    if r == 1 and isinstance(g, int) and g == GROUPS - 2:
                        one_hots(GROUPS - 1, 1 - s)

                def tail(r=r):
                    s = TAIL_SLOT
                    dve.wait_ge(s_seg[r], GROUPS + 1)
                    dve.tensor_tensor(onehot[0:TAIL, s, 0, :], iota_ps[0:TAIL, :],
                                      rel[0:TAIL, COLS - 1:COLS].to_broadcast([TAIL, WIN]),
                                      ALU.is_equal).then_inc(s_oh[r], 1)
                    if r == 0:
                        dve.wait_ge(s_gath[0][s], 16 * TILES * (IN_SLOT - early_in_slot(0, s)) + 16)
                        dve.wait_ge(s_edge_ps, GROUPS + 1)
                        dve.tensor_tensor(msg[0:TAIL, s, 0, 0:D], gath[0:TAIL, s, 0, :],
                                          edg_ps[0:TAIL, 0, 0:D], ALU.mult).then_inc(s_msg, 1)
                    add_window(GROUPS, s)

                def step(k, n, c, s, tiles, r=r):
                    added = c * PERIOD + PERIOD + 1
                    if isinstance(c, int) and c >= CHUNKS - 2:
                        added = GROUPS - 1 if c == CHUNKS - 2 else GROUPS + 1
                    (node_stage_0, node_stage_1)[r](dve, k, n, c, s, tiles, added)

                def step_again(k, n, c, s, tiles, r=r):
                    (node_stage_0, node_stage_1)[r](dve, k, n, c, s, tiles, GROUPS + 1)

                if r == 1:
                    dve.wait_ge(s_root, CHUNKS + SLOTS)
                go_round(dve, group, tail, step, AHEAD[r])
                with dve.If_ne(flag_reg, 0):
                    leftover_dve(dve, r, rows)
                    again(dve, step_again)
                    if r == 0:
                        dve.wait_ge(s_root, 2 * CHUNKS + SLOTS)

        @block.tensor
        def _(pe):
            pe.sem_inc(s_seg[0], SLOTS)
            pe.sem_inc(s_seg[1], SLOTS)
            pe.wait_ge(s_wpre, 32)

            def product(bank, left_T, w, tiles):
                for t in range(tiles):
                    last = pe.matmul(bank[:, t * D:(t + 1) * D], left_T[:, t * P:(t + 1) * P], w[:],
                                     start=True, stop=True)
                return last

            for c in range(CHUNKS):
                tiles = CT if c < CHUNKS - 1 else 1
                if c == CHUNKS - 2:
                    pe.wait_ge(s_ext, 2)
                    pe.wait_ge(s_const, 1)
                    for q in range(3):
                        last = pe.transpose(bank_a[0:1, q * P:(q + 1) * P], extent[:, 3 + q:4 + q], ident[:])
                    last.then_inc(s_extT, 1)
                if c in XT_AT:
                    pe.wait_ge(s_xT[XT_AT.index(c)], 16)
                    pe.wait_ge(s_ones, XT_AT.index(c) + 1)
                pe.wait_ge(s_h, c + 1)
                product((bank_b, bank_c)[c % 2], xT[:, c * CN:c * CN + tiles * P], w_pre, tiles
                        ).then_inc(s_hmm, 1)

            for b in range(BATCHES + 1):
                if b < BATCHES:
                    pe.wait_ge(s_xrows[b], 16 * len(batch(b)))
                    if b == 0:
                        pe.wait_ge(s_flag, 1)
                    else:
                        pe.wait_ge(s_xrows_kept, b)
                    for t, tile in enumerate(batch(b)):
                        last = pe.transpose(bank_a[0:D, t * P:(t + 1) * P], x2[:, tile, :], ident[:])
                    last.then_inc(s_xrows_turned, 1)
                if b > 0:
                    c = CHUNKS + b - 1
                    pe.wait_ge(s_h, c + 1)
                    pe.wait_ge(s_xrows_kept, b)
                    product((bank_b, bank_c)[c % 2], x2T[:, (b - 1) % SLOTS], w_pre, len(batch(b - 1))
                            ).then_inc(s_hmm, 1)

            flag_reg = left_flag(pe)
            pe.wait_ge(s_w, 8 * 16)
            pe.wait_ge(s_init, 1)

            def uses_before(n, tiles):
                return n + SLOTS if tiles == CT else n + 1

            def step_0(k, n, c, s, tiles):
                if k == 1:
                    pe.wait_ge(s_x1, n + 1)
                    pe.wait_ge(s_x2T, uses_before(n, tiles))
                    pe.matmul(area_a[tiles == 1][0:D, 0:tiles * P], w1[:], colsT[0:D, s, 0:tiles * P],
                              start=True, stop=True).then_inc(s_y1mm, 1)
                    pe.wait_ge(s_root, uses_before(n, tiles))
                    for t in range(tiles):
                        last = pe.transpose(area_c[tiles == 1][:, t * (D + 1):(t + 1) * (D + 1)],
                                            colsT[:, s, t * P:(t + 1) * P], ident[0:D + 1, 0:D + 1])
                    last.then_inc(s_x1n, 1)
                if k == 2:
                    pe.wait_ge(s_y1, n + 1)
                    pe.wait_ge(s_t, uses_before(n, tiles))
                    product(area_b[tiles == 1], y1[:, s], w2, tiles).then_inc(s_y2mm, 1)
                if k == 4:
                    pe.wait_ge(s_x2, n + 1)
                    for t in range(tiles):
                        last = pe.transpose(area_a[tiles == 1][0:D, t * P:(t + 1) * P], x2c[:, s, t, :], ident[:])
                    last.then_inc(s_x2t, 1)
                if k == 5:
                    pe.wait_ge(s_x2T, n + 1 + SLOTS)
                    product(area_b[tiles == 1], x2T[:, s], w_lin, tiles).then_inc(s_tmm, 1)
                if k == 6:
                    product(area_c[tiles == 1], x2T[:, s], w_root, tiles).then_inc(s_rmm, 1)

            def step_1(k, n, c, s, tiles):
                if k == 1:
                    pe.wait_ge(s_agg, n + 1)
                    pe.wait_ge(s_f1, uses_before(n, tiles))
                    for t in range(tiles):
                        last = pe.transpose(area_b[tiles == 1][:, t * D:(t + 1) * D],
                                            colsT[0:D, s, t * P:(t + 1) * P], ident[0:D, 0:D])
                    last.then_inc(s_aggn, 1)

            for r in range(2):
                rows = (D + 1, D)[r]
                values = (msg, gath)[r]

                def seg_sum(k, tiles, s, a=0, b=None, rows=rows, values=values):
                    for j in range(a, b or tiles):
                        last = pe.matmul(seg[0:rows, s, :], values[0:k, s, j, 0:rows],
                                         onehot[0:k, s, j, :], start=(j == 0), stop=(j == tiles - 1))
                    return last

                def group(g, s, r=r, seg_sum=seg_sum):
                    pe.wait_ge(s_oh[r], g + 1)
                    if isinstance(g, int) and g == GROUPS - 1:
                        pe.wait_ge(s_add[r], g + 1)
                        for q, (a, b) in enumerate(PARTS):
                            if r == 1:
                                pe.wait_ge(s_part[1][q], 16 * (b - a))
                            elif b < TILES:
                                pe.wait_ge(s_msg_part, q + 1)
                            else:
                                pe.wait_ge(s_msg, g + 1 + SLOTS)
                            last = seg_sum(P, TILES, s, a, b)
                        last.then_inc(s_seg[r], 1)
                        return
                    if r == 0:
                        pe.wait_ge(s_msg, g + 1 + SLOTS)
                    else:
                        pe.wait_ge(s_gath[1][s], landed(1, g, s))
                    pe.wait_ge(s_add[r], g + 1)
                    seg_sum(P, TILES, s).then_inc(s_seg[r], 1)

                def tail(r=r, seg_sum=seg_sum):
                    pe.wait_ge(s_oh[r], GROUPS + 1)
                    if r == 0:
                        pe.wait_ge(s_msg, GROUPS + 1 + SLOTS)
                    else:
                        pe.wait_ge(s_gath[1][TAIL_SLOT], 16 * TILES * IN_SLOT + 16)
                    pe.wait_ge(s_add[r], GROUPS + 1)
                    seg_sum(TAIL, 1, TAIL_SLOT).then_inc(s_seg[r], 1)

                def left_group(g, k, tiles, r=r, seg_sum=seg_sum):
                    with pe.Fori(0, WINDOWS) as w:
                        if r == 0:
                            pe.wait_ge(s_lmsg, g + 2)
                        else:
                            pe.wait_ge(s_lgath[1], g * (16 * TILES) + 16 * tiles)
                        pe.wait_ge(s_loh[r], g * WINDOWS + w + 1)
                        pe.wait_ge(s_ladd[r], g * WINDOWS + w + 1)
                        seg_sum(k, tiles, 0).then_inc(s_lseg[r], 1)

                go_round(pe, group, tail, (step_0, step_1)[r], AHEAD[r])
                with pe.If_ne(flag_reg, 0):
                    with pe.Fori(0, GROUPS) as g:
                        left_group(g, P, TILES)
                    left_group(GROUPS, TAIL, 1)
                    again(pe, (step_0, step_1)[r])


def kernel(**inputs):
    import numpy as np
    import concourse.bacc as bacc
    from concourse.bass_utils import run_bass_kernel_spmd

    a = {k: np.asarray(v) for k, v in inputs.items()}

    def edge_columns(e):
        body = e[:GROUPS * GROUP].reshape(GROUPS, P, TILES).transpose(1, 0, 2).reshape(P, GROUPS * TILES)
        return body, e[GROUPS * GROUP:].reshape(TAIL, 1)

    src_body, src_tail = edge_columns(a["src"])
    dst_body, dst_tail = edge_columns(a["dst"])
    arrays = {
        "x": a["x"], "xT": a["x"].T,
        "src_body": src_body, "src_tail": src_tail, "dst_body": dst_body, "dst_tail": dst_tail,
        "first": a["dst"][::GROUP],
        "edge": a["edge_attr_96"],
        "W_pre": a["L0_gnn_W_pre"], "b_pre": a["L0_gnn_b_pre"].reshape(1, D),
        "W1": a["L0_gnn_W1"], "b1": a["L0_gnn_b1"].reshape(D, 1),
        "W2": a["L0_gnn_W2"], "b2": a["L0_gnn_b2"].reshape(1, D),
        "WlinT": a["L1_gnn_W_lin"].T, "b_lin": a["L1_gnn_b_lin"].reshape(1, D),
        "WrootT": a["L1_gnn_W_root"].T, "b_root": a["L1_gnn_b_root"].reshape(1, D),
    }
    arrays = {k: np.ascontiguousarray(v) for k, v in arrays.items()}
    nc = bacc.Bacc("TRN2", target_bir_lowering=False, num_devices=1)
    d = {k: nc.dram_tensor(f"in_{k}", v.shape, mybir.dt.from_np(v.dtype), kind="ExternalInput").ap()
         for k, v in arrays.items()}
    out = nc.dram_tensor("out_y", (N_NODES, D), F32, kind="ExternalOutput").ap()
    build(nc, d["x"], d["xT"], (d["src_body"], d["src_tail"]), (d["dst_body"], d["dst_tail"]),
          d["first"], d["edge"], d["W_pre"], d["b_pre"], d["W1"], d["b1"], d["W2"], d["b2"],
          d["WlinT"], d["b_lin"], d["WrootT"], d["b_root"], out)
    r = run_bass_kernel_spmd(nc, [{f"in_{k}": v for k, v in arrays.items()}], core_ids=[0])
    return r.results[0]["out_y"]
```
